# Optimizing a Trainium2 kernel written in Bass

```python
import numpy as np
import jax
import jax.numpy as jnp

def _softmax(x, axis=-1):
    return jax.nn.softmax(x, axis=axis)

def _gelu(x):
    return jax.nn.gelu(x, approximate=True)

def _silu(x):
    return jax.nn.silu(x)

def _sigmoid(x):
    return jax.nn.sigmoid(x)

def _layernorm(x, axis=-1, eps=1e-05):
    m = jnp.mean(x, axis=axis, keepdims=True)
    v = jnp.var(x, axis=axis, keepdims=True)
    return (x - m) / jnp.sqrt(v + eps)

def _scatter_add(tgt, idx, src, axis=0):
    return tgt.at[idx].add(src)

def _segment_sum(src, seg, n):
    return jax.ops.segment_sum(src, seg, n)
kernel_name = 'mk_vit_tower_postln_d1_tok_img1024_r4_da2188'

def setup_inputs(seed: int=0):
    np.random.seed(seed)
    _w = jnp.asarray

    def _rec_inputs():
        import jax
        import jax.numpy as jnp
        _rk = jax.random.key(seed)
        x = -0.00016672 + 0.999947 * jax.random.normal(jax.random.fold_in(_rk, 1), (16, 3, 96, 96), jnp.float32)
        return x
    x = _rec_inputs()

    def _L0_tok_setup():
        import jax, jax.numpy as jnp
        import numpy as np
        P = 16

        def _patchify(x):
            B, C, H, W = x.shape
            gh, gw = (H // P, W // P)
            x = x.reshape(B, C, gh, P, gw, P)
            x = x.transpose(0, 2, 4, 1, 3, 5)
            return x.reshape(B, gh * gw, C * P * P)
        key = jax.random.key(seed)
        k1, k2, k3, k4, k5 = jax.random.split(key, 5)
        B, C, S = (64, 3, 96)
        lin_in, lout = (P * P * C, 256)
        n_patches = (S // P) ** 2
        return {'x': jax.random.normal(k1, (B, C, S, S), dtype=jnp.float32), 'W': jax.random.normal(k2, (lout, lin_in), dtype=jnp.float32) * 0.02, 'b': jax.random.normal(k3, (lout,), dtype=jnp.float32) * 0.02, 'class_token': jax.random.normal(k4, (1, 1, lout), dtype=jnp.float32) * 0.02, 'pos_embedding': jax.random.normal(k5, (1, n_patches + 1, lout), dtype=jnp.float32) * 0.02}
    _L0_tok_all = _L0_tok_setup()
    _L0_tok_in = {k: v for k, v in _L0_tok_all.items() if k in ('W', 'b', 'class_token', 'pos_embedding')}
    del _L0_tok_all

    def _L0_attn_setup():
        import jax, jax.numpy as jnp
        import numpy as np
        THETA = 10000.0

        def _rope(t):
            T, d = (t.shape[-2], t.shape[-1])
            freqs = 1.0 / THETA ** (jnp.arange(0, d, 2, dtype=jnp.float32) / d)
            ang = jnp.arange(T, dtype=jnp.float32)[:, None] * freqs[None, :]
            ang = jnp.repeat(ang, 2, axis=-1)
            cos, sin = (jnp.cos(ang), jnp.sin(ang))
            x = t.reshape(t.shape[:-1] + (d // 2, 2))
            x1, x2 = (x[..., 0], x[..., 1])
            rot = jnp.stack([-x2, x1], axis=-1).reshape(t.shape)
            return t * cos + rot * sin
        key = jax.random.key(seed)
        ks = jax.random.split(key, 5)
        B, T, C = (4, 512, 256)
        s = 0.02
        return {'x': jax.random.normal(ks[0], (B, T, C), dtype=jnp.float32), 'Wq': jax.random.normal(ks[1], (C, C), dtype=jnp.float32) * s, 'bq': jnp.zeros((C,), dtype=jnp.float32), 'Wk': jax.random.normal(ks[2], (C, C), dtype=jnp.float32) * s, 'bk': jnp.zeros((C,), dtype=jnp.float32), 'Wv': jax.random.normal(ks[3], (C, C), dtype=jnp.float32) * s, 'bv': jnp.zeros((C,), dtype=jnp.float32), 'Wf': jax.random.normal(ks[4], (C, C), dtype=jnp.float32) * s, 'bf': jnp.zeros((C,), dtype=jnp.float32)}
    _L0_attn_all = _L0_attn_setup()
    _L0_attn_in = {k: v for k, v in _L0_attn_all.items() if k in ('Wq', 'bq', 'Wk', 'bk', 'Wv', 'bv', 'Wf', 'bf')}
    del _L0_attn_all

    def _L0_ffn_setup():
        import jax, jax.numpy as jnp
        import numpy as np
        W_SCALE = 0.02
        TOP_K = 2
        key = jax.random.key(seed)
        ks = jax.random.split(key, 5)
        B, S, H, I, E = (2, 256, 256, 1024, 8)
        return {'x': jax.random.normal(ks[0], (B, S, H), dtype=jnp.float32), 'gate': jax.random.normal(ks[1], (H, E), dtype=jnp.float32) * W_SCALE, 'experts_w1': jax.random.normal(ks[2], (E, H, I), dtype=jnp.float32) * W_SCALE, 'experts_w2': jax.random.normal(ks[3], (E, I, H), dtype=jnp.float32) * W_SCALE, 'experts_w3': jax.random.normal(ks[4], (E, H, I), dtype=jnp.float32) * W_SCALE}
    _L0_ffn_all = _L0_ffn_setup()
    _L0_ffn_in = {k: v for k, v in _L0_ffn_all.items() if k in ('gate', 'experts_w1', 'experts_w2', 'experts_w3')}
    del _L0_ffn_all
    return {'x': x, 'L0_tok_W': _L0_tok_in['W'], 'L0_tok_b': _L0_tok_in['b'], 'L0_tok_class_token': _L0_tok_in['class_token'], 'L0_tok_pos_embedding': _L0_tok_in['pos_embedding'], 'L0_attn_Wq': _L0_attn_in['Wq'], 'L0_attn_bq': _L0_attn_in['bq'], 'L0_attn_Wk': _L0_attn_in['Wk'], 'L0_attn_bk': _L0_attn_in['bk'], 'L0_attn_Wv': _L0_attn_in['Wv'], 'L0_attn_bv': _L0_attn_in['bv'], 'L0_attn_Wf': _L0_attn_in['Wf'], 'L0_attn_bf': _L0_attn_in['bf'], 'L0_ffn_gate': _L0_ffn_in['gate'], 'L0_ffn_experts_w1': _L0_ffn_in['experts_w1'], 'L0_ffn_experts_w2': _L0_ffn_in['experts_w2'], 'L0_ffn_experts_w3': _L0_ffn_in['experts_w3']}

def reference(x, L0_tok_W, L0_tok_b, L0_tok_class_token, L0_tok_pos_embedding, L0_attn_Wq, L0_attn_bq, L0_attn_Wk, L0_attn_bk, L0_attn_Wv, L0_attn_bv, L0_attn_Wf, L0_attn_bf, L0_ffn_gate, L0_ffn_experts_w1, L0_ffn_experts_w2, L0_ffn_experts_w3):
    import jax
    import jax.numpy as jnp

    def _L0_tok_ref(x, W, b, class_token, pos_embedding):
        import jax, jax.numpy as jnp
        import numpy as np
        P = 16

        def _patchify(x):
            B, C, H, W = x.shape
            gh, gw = (H // P, W // P)
            x = x.reshape(B, C, gh, P, gw, P)
            x = x.transpose(0, 2, 4, 1, 3, 5)
            return x.reshape(B, gh * gw, C * P * P)
        patches = _patchify(x)
        proj = jnp.einsum('bnk,dk->bnd', patches, W) + b
        B = x.shape[0]
        cls = jnp.broadcast_to(class_token, (B, 1, proj.shape[-1]))
        out = jnp.concatenate([cls, proj], axis=1) + pos_embedding
        return out

    def _L0_attn_ref(x, Wq, bq, Wk, bk, Wv, bv, Wf, bf):
        import jax, jax.numpy as jnp
        import numpy as np
        THETA = 10000.0

        def _rope(t):
            T, d = (t.shape[-2], t.shape[-1])
            freqs = 1.0 / THETA ** (jnp.arange(0, d, 2, dtype=jnp.float32) / d)
            ang = jnp.arange(T, dtype=jnp.float32)[:, None] * freqs[None, :]
            ang = jnp.repeat(ang, 2, axis=-1)
            cos, sin = (jnp.cos(ang), jnp.sin(ang))
            x = t.reshape(t.shape[:-1] + (d // 2, 2))
            x1, x2 = (x[..., 0], x[..., 1])
            rot = jnp.stack([-x2, x1], axis=-1).reshape(t.shape)
            return t * cos + rot * sin
        B, T, C = x.shape
        Q = _rope(x @ Wq.T + bq)
        K = _rope(x @ Wk.T + bk)
        V = x @ Wv.T + bv
        A = jnp.einsum('btd,bsd->bts', Q, K) / jnp.sqrt(jnp.float32(C))
        causal = jnp.tril(jnp.ones((T, T), dtype=bool))
        A = jnp.where(causal, A, -jnp.inf)
        A = jax.nn.softmax(A, axis=-1)
        out = jnp.einsum('bts,bsd->btd', A, V)
        return out @ Wf.T + bf

    def _L0_ffn_ref(x, gate, experts_w1, experts_w2, experts_w3):
        import jax, jax.numpy as jnp
        import numpy as np
        W_SCALE = 0.02
        TOP_K = 2
        E = experts_w1.shape[0]
        router_logits = jnp.einsum('bsh,he->bse', x, gate)
        routing_weights, selected = jax.lax.top_k(router_logits, TOP_K)
        routing_weights = jax.nn.softmax(routing_weights, axis=-1)
        onehot = jax.nn.one_hot(selected, E, dtype=x.dtype)
        tok_w = jnp.einsum('bsk,bske->bse', routing_weights, onehot)
        g = jnp.einsum('bsh,ehi->ebsi', x, experts_w1)
        u = jnp.einsum('bsh,ehi->ebsi', x, experts_w3)
        hid = jax.nn.silu(g) * u
        eo = jnp.einsum('ebsi,eih->ebsh', hid, experts_w2)
        out = jnp.einsum('ebsh,bse->bsh', eo, tok_w)
        return out
    h = _L0_tok_ref(x, L0_tok_W, L0_tok_b, L0_tok_class_token, L0_tok_pos_embedding)
    h = _layernorm(h + _L0_attn_ref(h, L0_attn_Wq, L0_attn_bq, L0_attn_Wk, L0_attn_bk, L0_attn_Wv, L0_attn_bv, L0_attn_Wf, L0_attn_bf), axis=-1)
    h = _layernorm(h + _L0_ffn_ref(h, L0_ffn_gate, L0_ffn_experts_w1, L0_ffn_experts_w2, L0_ffn_experts_w3), axis=-1)
    return h

_drawn_inputs = setup_inputs


def setup_inputs(seed=0):
    import zlib

    import numpy as np

    out = dict(_drawn_inputs(seed))
    spreads = {'L0_attn_bq': (0.0, 0.8),
     'L0_attn_bk': (0.0, 2.0),
     'L0_attn_bv': (0.0, 0.1),
     'L0_attn_bf': (0.0, 0.1)}
    factors = {'L0_attn_Wq': 8.0, 'L0_attn_Wk': 8.0, 'L0_ffn_gate': 2.715}
    for name, (base, spread) in spreads.items():
        noise = np.random.default_rng([zlib.crc32(name.encode()), seed]).standard_normal(out[name].shape)
        drawn = base * np.exp(spread * noise) if base else spread * noise
        out[name] = jnp.asarray(drawn.astype(out[name].dtype))
    for name, factor in factors.items():
        out[name] = (out[name] * factor).astype(out[name].dtype)
    return out
```

```python
from contextlib import ExitStack

import numpy as np

import concourse.bass as bass
from concourse import mybir

ALU = mybir.AluOpType
ACT = mybir.ActivationFunctionType
AX_X = mybir.AxisListType.X
F32 = mybir.dt.float32
F32R = mybir.dt.float32r
BF16 = mybir.dt.bfloat16
U32 = mybir.dt.uint32
I32 = mybir.dt.int32

B, CH, IMG, PATCH = 16, 3, 96, 16
GRID = IMG // PATCH
NP = GRID * GRID
T = NP + 1
TOK = B * T
D = 256
DT = D // 128
KP = CH * PATCH * PATCH // 128
HALF_B = B // 2
HALF_P, HALF_T = HALF_B * NP, HALF_B * T
GB = 128 // T
GT = GB * T
NG = -(-B // GB)
GROUP = [min(GT, TOK - g * GT) for g in range(NG)]
E, INNER = 8, 1024
MT = INNER // 128
SLOTS = 208
ST = 2
SLOT_T = SLOTS // ST
PASSES = -(-TOK // SLOTS)
PASS_ROWS = E * SLOTS
EPS = 1e-5
NEG = -1e30
WCH = 2 * DT * INNER // MT

C_ID = 0
C_MASK = C_ID + 128
C_TRI = C_MASK + GT
C_COS = C_TRI + GT
C_SIN = C_COS + T
C_IOTA = C_SIN + T
C_ROW0 = C_IOTA + SLOTS
C_LT = C_ROW0 + E
C_TID = C_LT + E * E
C_W = C_TID + 2 * NG

V_BQ, V_BK, V_BT, V_CLS, V_POS = 0, DT, 2 * DT, 3 * DT, 4 * DT
V_W = V_POS + DT * T


def shape_constants():
    c = np.zeros((128, C_W), np.float32)
    c[:, C_ID:C_ID + 128] = np.eye(128)
    p, q = np.arange(GT)[:, None], np.arange(GT)[None, :]
    c[:GT, C_MASK:C_MASK + GT] = np.where((p // T == q // T) & (q <= p), 0.0, NEG)
    c[:GT, C_TRI:C_TRI + GT] = p < q
    freqs = (np.float32(1.0) / np.float32(10000.0) ** (np.arange(0, D, 2, dtype=np.float32) / np.float32(D)))
    ang = freqs.astype(np.float32)[:, None] * np.arange(T, dtype=np.float32)[None, :]
    c[:, C_COS:C_COS + T] = np.cos(ang)
    c[:, C_SIN:C_SIN + T] = np.sin(ang)
    c[:, C_IOTA:C_IOTA + SLOTS] = np.arange(SLOTS)
    c[:, C_ROW0:C_ROW0 + E] = np.arange(E) * SLOTS
    e, f = np.arange(E)[:, None], np.arange(E)[None, :]
    c[:, C_LT:C_LT + E * E] = (f < e).reshape(-1)
    for g in range(NG):
        token = g * GT + np.arange(128)
        c[:, C_TID + 2 * g] = token // 4 * 4
        c[:, C_TID + 2 * g + 1] = token % 4
    return c


def vit_layer(nc, patches, tok_w, vecs, attn_w, bv, bf, gate, w1, w3, w2, consts, out):
    h1_dram = nc.dram_tensor("h1_rows", (TOK, D), F32, kind="Internal").ap()
    y_dram = nc.dram_tensor("expert_rows", (PASSES * PASS_ROWS, D), F32, kind="Internal").ap()
    out_rows = out.rearrange("b j d -> (b j) d")

    with ExitStack() as ctx:
        def sb(name, shape, dt=F32):
            return ctx.enter_context(nc.sbuf_tensor(name, shape, dt))

        def sem(name):
            return ctx.enter_context(nc.semaphore(name))

        bank = ctx.enter_context(nc.psum_tensor("bank", [128, 8, 512], F32))

        cst = sb("cst", [128, C_W])
        vec = sb("vec", [128, V_W])
        bv_rows = sb("bv_rows", [GT, D])
        bf_rows = sb("bf_rows", [GT, D])
        tok_w_sb = sb("tok_w_sb", [128, KP, D])
        patch_sb = sb("patch_sb", [128, 2, KP, HALF_P])
        attn_w_sb = sb("attn_w_sb", [128, 4, DT, D])
        gate_sb = sb("gate_sb", [128, DT, E])
        ident = cst[:, C_ID:C_ID + 128]
        mask = cst[0:GT, C_MASK:C_MASK + GT]
        iota = cst[0:GT, C_IOTA:C_IOTA + SLOTS]
        row0 = cst[0:GT, C_ROW0:C_ROW0 + E]
        lower = cst[0:GT, C_LT:C_LT + E * E].rearrange("p (e f) -> p e f", e=E)
        tri_b = sb("tri_b", [GT, GT], BF16)
        ones_b = sb("ones_b", [GT, GT], BF16)
        tid_b = sb("tid_b", [GT, NG, 2], BF16)

        posb = sb("posb", [128, DT, T])
        hT = sb("hT", [128, DT, TOK])
        rope_t = sb("rope_t", [128, 2, 4, HALF_T])
        qk = sb("qk", [128, 2, 2, TOK])
        v_sb = sb("v_sb", [GT, NG, D])
        resid = sb("resid", [GT, NG, D])
        score = sb("score", [GT, 2, GT])
        prob = sb("prob", [GT, 2, GT])
        probT = sb("probT", [GT, 2, GT])
        attnT = sb("attnT", [128, 2, DT, GT])
        top = sb("top", [GT, NG])
        neg_top = sb("neg_top", [GT, NG])
        prob_sum = sb("prob_sum", [GT, NG])
        prob_inv = sb("prob_inv", [GT, NG])
        pre = sb("pre", [GT, NG, D])
        stats = sb("stats", [GT, NG, 6])
        mv = sb("mv", [GT, NG, 2])
        std = sb("std", [GT, NG])
        eps_col = sb("eps_col", [GT, 1])
        rstd = sb("rstd", [GT, NG])
        h1 = tok_w_sb[0:GT]
        h1T = attn_w_sb[:].rearrange("p a k d -> p (a k d)")[:, 0:NG * DT * GT].rearrange("p (g k t) -> p g k t", g=NG, k=DT)

        logit = sb("logit", [GT, NG, E])
        qk_flat = qk[0:GT].rearrange("p a b t -> p (a b t)")
        above = qk_flat[:, 0:NG * E * E].rearrange("p (g e f) -> p g e f", g=NG, e=E)
        equal = qk_flat[:, NG * E * E:2 * NG * E * E].rearrange("p (g e f) -> p g e f", g=NG, e=E)
        rank = sb("rank", [GT, NG, E])
        picked = sb("picked", [GT, NG, E])
        picked_b = sb("picked_b", [GT, NG, E], BF16)
        first = sb("first", [GT, NG, E])
        second = sb("second", [GT, NG, E])
        pos = sb("pos", [GT, NG, E])
        pos1 = sb("pos1", [GT, NG, E])
        slot_of = sb("slot_of", [GT, E, NG])
        row_of = sb("row_of", [GT, NG, E])
        pick_t = sb("pick_t", [GT, 4, NG, E])
        row_idx = sb("row_idx", [GT, 2, NG], U32)
        most = sb("most", [1, 1], I32)
        l1 = sb("l1", [GT, NG])
        l2 = sb("l2", [GT, NG])
        gap = sb("gap", [GT, NG])
        tanh_gap = sb("tanh_gap", [GT, NG])
        route_w = sb("route_w", [GT, 2, NG])
        sel = sb("sel", [GT, NG, SLOTS], BF16)
        tok_idx = sb("tok_idx", [SLOT_T, 2, ST, 1], U32)

        raw = sb("raw", [128, 2, 2, DT * INNER])
        w2_sb = sb("w2_sb", [128, 2, MT, D])
        w_hi = sb("w_hi", [128, 2, 2 * DT * INNER], F32R)
        w_lo = sb("w_lo", [128, 2, 2 * DT * INNER], F32R)
        rope_flat = rope_t[:].rearrange("p a b t -> p (a b t)")
        XG_W, GATED_W = 2 * ST * D, 2 * SLOTS
        xg = rope_flat[0:SLOT_T, 0:XG_W].rearrange("p (b t d) -> p b t d", b=2, t=ST)
        gated = rope_flat[:, XG_W:XG_W + GATED_W].rearrange("p (b t) -> p b t", b=2)
        yT = rope_flat[:, XG_W + GATED_W:XG_W + GATED_W + DT * SLOTS].rearrange("p (m t) -> p m t", m=DT)
        x_hi = sb("x_hi", [128, 2, DT, SLOTS], F32R)
        x_lo = sb("x_lo", [128, 2, DT, SLOTS], F32R)
        hid = patch_sb[:].rearrange("p a k t -> p (a k t)")[:, 0:2 * MT * SLOTS].rearrange("p (b m t) -> p b m t", b=2, m=MT)
        y_sb = hT[0:SLOT_T].rearrange("p k t -> p (k t)")[:, 0:2 * ST * D].rearrange("p (b t d) -> p b t d", b=2, t=ST)
        rows_w = NG * D
        raw_flat = raw[0:GT].rearrange("p a b c -> p (a b c)")
        y_tok = raw_flat[:, 0:2 * rows_w].rearrange("p (k g d) -> p k g d", k=2, g=NG)
        mix, mix2, out_sb = (raw_flat[:, j * rows_w:(j + 1) * rows_w].rearrange("p (g d) -> p g d", g=NG) for j in (2, 3, 4))

        s_front = [sem(f"s_front{k}") for k in range(KP // 2)]
        s_patch1 = sem("s_patch1")
        s_small = sem("s_small")
        s_attn_w = sem("s_attn_w")
        s_bias = sem("s_bias")
        s_w1 = [sem(f"s_w1_{p}") for p in range(2)]
        s_w3 = [sem(f"s_w3_{p}") for p in range(2)]
        s_w2 = [sem(f"s_w2_{p}") for p in range(2)]
        s_setup = sem("s_setup")
        s_link = sem("s_link")
        s_tri = sem("s_tri")
        s_patch_mm = sem("s_patch_mm")
        s_hT = sem("s_hT")
        s_qk_mm = sem("s_qk_mm")
        s_rope_mul = sem("s_rope_mul")
        s_rope = sem("s_rope")
        s_vh_mm = sem("s_vh_mm")
        s_vh = sem("s_vh")
        s_score_mm = sem("s_score_mm")
        s_score = sem("s_score")
        s_neg_top = sem("s_neg_top")
        s_prob = sem("s_prob")
        s_probT_mm = sem("s_probT_mm")
        s_probT = sem("s_probT")
        s_attn_mm = sem("s_attn_mm")
        s_attn = sem("s_attn")
        s_proj_mm = sem("s_proj_mm")
        s_pre = sem("s_pre")
        s_mv = sem("s_mv")
        s_std = sem("s_std")
        s_h1 = sem("s_h1")
        s_h1_dram = sem("s_h1_dram")
        s_h1T_mm = sem("s_h1T_mm")
        s_h1T = sem("s_h1T")
        s_logit_mm = sem("s_logit_mm")
        s_picked = sem("s_picked")
        s_pos_mm = sem("s_pos_mm")
        s_pos = sem("s_pos")
        s_row_idx = sem("s_row_idx")
        s_gap = sem("s_gap")
        s_tanh = sem("s_tanh")
        s_sel = sem("s_sel")
        s_idx_mm = sem("s_idx_mm")
        s_idx = sem("s_idx")
        s_gathers = sem("s_gathers")
        s_xg = [sem(f"s_xg{p}") for p in range(2)]
        s_xT_mm = sem("s_xT_mm")
        s_xh = sem("s_xh")
        s_x = sem("s_x")
        s_whi = sem("s_whi")
        s_wlo = sem("s_wlo")
        s_gu_mm = sem("s_gu_mm")
        s_silu = sem("s_silu")
        s_hid = sem("s_hid")
        s_y_mm = sem("s_y_mm")
        s_y = sem("s_y")
        s_yT_mm = sem("s_yT_mm")
        s_yr = sem("s_yr")
        s_y_dram = [sem(f"s_y_dram{p}") for p in range(2)]
        s_y_tok = [sem(f"s_y_tok{g}") for g in range(NG)]
        s_mv2 = sem("s_mv2")
        s_std2 = sem("s_std2")
        s_out = sem("s_out")
        s_out_dram = sem("s_out_dram")
        o_w = sem("o_w")
        o_slot = sem("o_slot")
        o_sel = sem("o_sel")
        o_idx_mm = sem("o_idx_mm")
        o_idx = sem("o_idx")
        o_xg = sem("o_xg")
        o_xT_mm = sem("o_xT_mm")
        o_x = sem("o_x")
        o_gu_mm = sem("o_gu_mm")
        o_silu = sem("o_silu")
        o_hid = sem("o_hid")
        o_y_mm = sem("o_y_mm")
        o_y = sem("o_y")
        o_yT_mm = sem("o_yT_mm")
        o_yr = sem("o_yr")
        o_y_dram = sem("o_y_dram")

        cos8 = cst[:, C_COS:C_COS + T].unsqueeze(1).broadcast_to([128, HALF_B, T])
        sin8 = cst[:, C_SIN:C_SIN + T].unsqueeze(1).broadcast_to([128, HALF_B, T])

        def per_image(ap, n):
            return ap.rearrange("p (b j) -> p b j", j=n)

        def further_passes(eng):
            return eng.If(eng.value_load(most[0:1, 0:1], min_val=0, max_val=TOK) > SLOTS)

        def whole_numbers():
            return nc.allow_low_precision(reason="sums of whole numbers below 2**24, kept as integers")

        MORE = PASSES - 1
        x_o = hid[:, 1, 0:DT, :]

        block = ctx.enter_context(nc.Block())

        def all_stored(eng):
            for par in range(2):
                eng.wait_ge(s_y_dram[par], 16 * (E // 2))

        @block.sync
        def _(sp):
            for k in range(KP // 2):
                sp.dma_start(tok_w_sb[:, 2 * k:2 * k + 2, :], tok_w[k]).then_inc(s_front[k], 16)
                sp.dma_start(patch_sb[:, 0, 2 * k:2 * k + 2, :], patches[0, k]).then_inc(s_front[k], 16)
            for k in range(KP // 2):
                sp.dma_start(patch_sb[:, 1, 2 * k:2 * k + 2, :], patches[1, k]).then_inc(s_patch1, 16)
            sp.dma_start(attn_w_sb[:], attn_w).then_inc(s_attn_w, 16)
            for par in range(2):
                sp.dma_start(raw[:, par, 0, :], w1[par]).then_inc(s_w1[par], 16)
                sp.dma_start(raw[:, par, 1, :], w3[par]).then_inc(s_w3[par], 16)
                sp.dma_start(w2_sb[:, par], w2[par]).then_inc(s_w2[par], 16)
            for g in range(NG):
                sp.wait_ge(s_h1, g + 1)
                sp.dma_start(h1_dram[g * GT:g * GT + GROUP[g], :], h1[0:GROUP[g], g, :]).then_inc(s_h1_dram, 16)

            def store(e, par):
                row = sp.snap(e * SLOTS)
                sp.wait_ge(s_yr, e + 1)
                sp.dma_start(y_dram[bass.ds(row, SLOTS), :].rearrange("(t p) d -> p t d", p=SLOT_T),
                             y_sb[:, par]).then_inc(s_y_dram[par], 16)

            def expert(i, par, load):
                e = 2 * i + par
                if load:
                    sp.wait_ge(s_wlo, MT * e + MT)
                    sp.dma_start(raw[:, par, 0, :], w1[bass.ds(e + 2, 1)].rearrange("o p c -> (o p) c")).then_inc(s_w1[par], 16)
                    sp.dma_start(raw[:, par, 1, :], w3[bass.ds(e + 2, 1)].rearrange("o p c -> (o p) c")).then_inc(s_w3[par], 16)
                    sp.wait_ge(s_y_mm, e + 1)
                    sp.dma_start(w2_sb[:, par], w2[bass.ds(e + 2, 1)].rearrange("o p m d -> (o p) m d")).then_inc(s_w2[par], 16)
                store(e, par)

            with sp.Fori(0, E // 2 - 1) as i:
                for par in range(2):
                    expert(i, par, True)
            for par in range(2):
                expert(E // 2 - 1, par, False)

            sp.wait_ge(s_row_idx, 1)
            with further_passes(sp):
                with sp.Fori(0, E) as e:
                    for c in range(MORE):
                        n = e * MORE + c
                        all_stored(sp)
                        sp.dma_start(raw[:, 0, 0, :], w1[bass.ds(e, 1)].rearrange("o p c -> (o p) c")).then_inc(o_w, 16)
                        sp.dma_start(raw[:, 0, 1, :], w3[bass.ds(e, 1)].rearrange("o p c -> (o p) c")).then_inc(o_w, 16)
                        sp.dma_start(w2_sb[:, 0], w2[bass.ds(e, 1)].rearrange("o p m d -> (o p) m d")).then_inc(o_w, 16)
                        row = sp.snap(e * SLOTS + (c + 1) * PASS_ROWS)
                        sp.wait_ge(o_yr, n + 1)
                        sp.dma_start(y_dram[bass.ds(row, SLOTS), :].rearrange("(t p) d -> p t d", p=SLOT_T),
                                     y_sb[:, 0]).then_inc(o_y_dram, 16)
                sp.wait_ge(o_y_dram, 16 * E * MORE)
            for g in range(NG):
                sp.wait_ge(s_out, g + 1)
                sp.dma_start(out_rows[g * GT:g * GT + GROUP[g], :], out_sb[0:GROUP[g], g, :]).then_inc(s_out_dram, 16)
            sp.wait_ge(s_out_dram, 16 * NG)
            sp.wait_ge(s_h1_dram, 16 * NG)

        @block.gpsimd
        def _(pool):
            pool.memset(ones_b[:], 1.0).then_inc(s_setup, 1)
            pool.memset(mv[:], 1.0).then_inc(s_setup, 1)
            pool.memset(logit[:], 0.0).then_inc(s_setup, 1)
            for half in range(2):
                for w in range(2):
                    n = 2 * half + w
                    cols = slice(half * HALF_T, (half + 1) * HALF_T)
                    pool.wait_ge(s_rope_mul, n + 1)
                    pool.tensor_tensor(qk[:, w, 0, cols], rope_t[:, n % 2, 0, :], rope_t[:, n % 2, 1, :], ALU.subtract)
                    pool.tensor_tensor(qk[:, w, 1, cols], rope_t[:, n % 2, 2, :], rope_t[:, n % 2, 3, :],
                                       ALU.add).then_inc(s_rope, 1)

            def gather(e, par):
                pool.wait_ge(s_idx, e + 1)
                pool.sem_inc(s_gathers, 1)
                for t in range(ST):
                    pool.indirect_dma_start(xg[:, par, t, :], None, h1_dram[:, :],
                                            bass.IndirectOffsetOnAxis(tok_idx[:, par, t, :], 0)).then_inc(s_xg[par], 16)

            pool.wait_ge(s_h1_dram, 16 * NG)
            for par in range(2):
                gather(par, par)
            with pool.Fori(0, E // 2 - 1) as i:
                for par in range(2):
                    e = 2 * i + par
                    pool.wait_ge(s_xT_mm, e + 1)
                    gather(e + 2, par)

            def token_rows(rows):
                for g in range(NG):
                    for k in range(2):
                        pool.indirect_dma_start(y_tok[0:GROUP[g], k, g, :], None, y_dram[0:rows, :],
                                                bass.IndirectOffsetOnAxis(row_idx[0:GROUP[g], k, g:g + 1], 0)).then_inc(s_y_tok[g], 16)

            pool.wait_ge(s_row_idx, 1)
            all_stored(pool)
            with further_passes(pool):
                with pool.Fori(0, E * MORE) as n:
                    pool.wait_ge(o_idx, n + 1)
                    pool.sem_inc(s_gathers, 1)
                    for t in range(ST):
                        pool.indirect_dma_start(xg[:, 0, t, :], None, h1_dram[:, :],
                                                bass.IndirectOffsetOnAxis(tok_idx[:, 0, t, :], 0)).then_inc(o_xg, 16)
                pool.wait_ge(o_y_dram, 16 * E * MORE)
                token_rows(PASSES * PASS_ROWS)
            with pool.Else():
                token_rows(PASS_ROWS)

        @block.tensor
        def _(pe):
            def exact3(dst, whi, wlo, xhi, xlo, start, stop):
                pe.matmul(dst, whi, xhi, start=start, stop=False)
                pe.matmul(dst, whi, xlo, start=False, stop=False)
                return pe.matmul(dst, wlo, xhi, start=False, stop=stop)

            for half in range(2):
                for k in range(KP):
                    if half == 0 and k % 2 == 0:
                        pe.wait_ge(s_front[k // 2], 32)
                    if half == 1 and k == 0:
                        pe.wait_ge(s_patch1, 16 * (KP // 2))
                    for m in range(DT):
                        last = pe.matmul(bank[:, 2 * half + m, 0:HALF_P], tok_w_sb[:, k, m * 128:(m + 1) * 128],
                                         patch_sb[:, half, k, :], start=(k == 0), stop=(k == KP - 1))
                last.then_inc(s_patch_mm, 1)
            pe.wait_ge(s_attn_w, 16)
            for half in range(2):
                pe.wait_ge(s_hT, 1 + DT * (half + 1))
                for w in range(2):
                    for eo in range(2):
                        for k in range(DT):
                            last = pe.matmul(bank[:, 4 * (1 - half) + 2 * w + eo, 0:HALF_T],
                                             attn_w_sb[:, w, k, eo * 128:(eo + 1) * 128],
                                             hT[:, k, half * HALF_T:(half + 1) * HALF_T], start=(k == 0), stop=(k == DT - 1))
                    last.then_inc(s_qk_mm, 1)

            def cols(g):
                return slice(g * GT, g * GT + GROUP[g])

            def values_and_rows(g):
                n = GROUP[g]
                if g < 2:
                    pe.wait_ge(s_rope_mul, 3)
                else:
                    pe.wait_ge(s_vh, g - 1)
                if g == 0:
                    pe.wait_ge(s_small, 32)
                for k in range(DT):
                    pe.matmul(bank[0:n, g % 2, 0:D], hT[:, k, cols(g)], attn_w_sb[:, 2, k, :], start=(k == 0), stop=(k == DT - 1))
                for k in range(DT):
                    last = pe.transpose(bank[0:n, g % 2, D + k * 128:D + (k + 1) * 128], hT[:, k, cols(g)], ident)
                last.then_inc(s_vh_mm, 1)

            def scores(g):
                n = GROUP[g]
                pe.wait_ge(s_rope, 2 if (g + 1) * GT <= HALF_T else 4)
                if g < 2:
                    pe.wait_ge(s_rope_mul, 4)
                else:
                    pe.wait_ge(s_score, g - 1)
                for eo in range(2):
                    last = pe.matmul(bank[0:n, 2 + g % 2, 0:n], qk[:, 0, eo, cols(g)], qk[:, 1, eo, cols(g)],
                                     start=(eo == 0), stop=(eo == 1))
                last.then_inc(s_score_mm, 1)

            for g in range(2):
                values_and_rows(g)
                scores(g)
            for g in range(NG):
                n = GROUP[g]
                pe.wait_ge(s_prob, g + 1)
                if g >= 2:
                    pe.wait_ge(s_probT, g - 1)
                pe.transpose(bank[0:n, 4 + g % 2, 0:n], prob[0:n, g % 2, 0:n], cst[0:n, C_ID:C_ID + n]).then_inc(s_probT_mm, 1)
                if g + 2 < NG:
                    values_and_rows(g + 2)
                pe.wait_ge(s_probT, g + 1)
                pe.wait_ge(s_vh, g + 1)
                if g >= 1:
                    pe.wait_ge(s_attn, g)
                for m in range(DT):
                    last = pe.matmul(bank[:, 6, m * 128:m * 128 + n], v_sb[0:n, g, m * 128:(m + 1) * 128],
                                     probT[0:n, g % 2, 0:n], start=True, stop=True)
                last.then_inc(s_attn_mm, 1)
                if g + 2 < NG:
                    scores(g + 2)
                pe.wait_ge(s_attn, g + 1)
                if g >= 1:
                    pe.wait_ge(s_pre, g)
                for k in range(DT):
                    last = pe.matmul(bank[0:n, 7, 0:D], attnT[:, g % 2, k, 0:n], attn_w_sb[:, 3, k, :],
                                     start=(k == 0), stop=(k == DT - 1))
                last.then_inc(s_proj_mm, 1)

            for g in range(NG):
                n = GROUP[g]
                pe.wait_ge(s_h1, g + 1)
                for k in range(DT):
                    last = pe.transpose(bank[:, g // 2, (g % 2 * DT + k) * 128:(g % 2 * DT + k) * 128 + n],
                                        h1[0:n, g, k * 128:(k + 1) * 128], cst[0:n, C_ID:C_ID + n])
                if g % 2 == 1:
                    last.then_inc(s_h1T_mm, 1)
            pe.wait_ge(s_bias, 48)
            for g in range(NG):
                n = GROUP[g]
                if g % 2 == 0:
                    pe.wait_ge(s_h1T, g // 2 + 1)
                for k in range(DT):
                    last = pe.matmul(bank[0:n, 3, g * E:(g + 1) * E], h1T[:, g, k, 0:n], gate_sb[:, k, :],
                                     start=(k == 0), stop=(k == DT - 1))
            last.then_inc(s_logit_mm, 1)
            pe.wait_ge(s_picked, 1)
            pe.wait_ge(s_tri, 2)
            for g in range(NG):
                n = GROUP[g]
                for j in range(g):
                    pe.matmul(bank[0:GT, 4, g * E:(g + 1) * E], ones_b[:], picked_b[:, j, :], start=(j == 0), stop=False)
                pe.matmul(bank[0:GT, 4, g * E:(g + 1) * E], tri_b[0:n, :], picked_b[0:n, g, :], start=(g == 0), stop=True)
            for g in range(NG):
                n = GROUP[g]
                last = pe.matmul(bank[0:GT, 4, NG * E:(NG + 1) * E], ones_b[0:n, :], picked_b[0:n, g, :],
                                 start=(g == 0), stop=(g == NG - 1))
            last.then_inc(s_pos_mm, 1)

            def slot_tokens():
                for t in range(ST):
                    for g in range(NG):
                        n = GROUP[g]
                        last = pe.matmul(bank[0:SLOT_T, 7, 2 * t:2 * t + 2], sel[0:n, g, t * SLOT_T:(t + 1) * SLOT_T],
                                         tid_b[0:n, g, :], start=(g == 0), stop=(g == NG - 1))
                return last

            def rows_transposed(par):
                for k in range(DT):
                    for t in range(ST):
                        last = pe.transpose(bank[:, 5, (k * ST + t) * SLOT_T:(k * ST + t + 1) * SLOT_T],
                                            xg[:, par, t, k * 128:(k + 1) * 128], cst[0:SLOT_T, C_ID:C_ID + SLOT_T])
                return last

            def y_rows():
                for t in range(ST):
                    for m in range(DT):
                        last = pe.transpose(bank[0:SLOT_T, 6, (t * DT + m) * 128:(t * DT + m + 1) * 128],
                                            yT[:, m, t * SLOT_T:(t + 1) * SLOT_T], ident)
                return last

            def w_at(w, par, which, k, m):
                c0 = (which * DT + k) * INNER + m * 128
                return w[:, par, c0:c0 + 128]

            for par in range(2):
                pe.wait_ge(s_sel, par + 1)
                if par == 1:
                    pe.wait_ge(s_idx, 1)
                slot_tokens().then_inc(s_idx_mm, 1)
            pe.wait_ge(s_xg[0], 16 * ST)
            rows_transposed(0).then_inc(s_xT_mm, 1)

            def expert(i, par, gather_next, next_rows, prev_rows):
                e = 2 * i + par
                pe.wait_ge(s_x, e + 1)
                pe.wait_ge(s_wlo, MT * e + MT)
                for m in range(MT):
                    if m < 4:
                        if prev_rows:
                            pe.wait_ge(s_hid, MT * e + m - 3)
                    else:
                        pe.wait_ge(s_hid, MT * e + m - 3)
                    for which in range(2):
                        for k in range(DT):
                            last = exact3(bank[:, m % 4, which * SLOTS:(which + 1) * SLOTS],
                                          w_at(w_hi, par, which, k, m), w_at(w_lo, par, which, k, m),
                                          x_hi[:, par, k, :], x_lo[:, par, k, :], k == 0, k == DT - 1)
                    last.then_inc(s_gu_mm, 1)
                    if m == 1 and prev_rows:
                        pe.wait_ge(s_y, e)
                        y_rows().then_inc(s_yT_mm, 1)
                    if m == 4 and gather_next:
                        pe.wait_ge(s_sel, e + 3)
                        slot_tokens().then_inc(s_idx_mm, 1)
                if next_rows:
                    pe.wait_ge(s_xg[1 - par], 16 * ST * (i + 1 + par))
                    rows_transposed(1 - par).then_inc(s_xT_mm, 1)
                pe.wait_ge(s_w2[par], 16 * (i + 1))
                if prev_rows:
                    pe.wait_ge(s_y, e)
                for m in range(DT):
                    for t in range(MT):
                        if m == 0:
                            pe.wait_ge(s_hid, MT * e + t + 1)
                        last = pe.matmul(bank[:, 4, m * SLOTS:(m + 1) * SLOTS], w2_sb[:, par, t, m * 128:(m + 1) * 128],
                                         hid[:, par, t, :], start=(t == 0), stop=(t == MT - 1))
                last.then_inc(s_y_mm, 1)

            expert(0, 0, True, True, False)
            expert(0, 1, True, True, True)
            with pe.Fori(1, E // 2 - 1) as i:
                for par in range(2):
                    expert(i, par, True, True, True)
            expert(E // 2 - 1, 0, False, True, True)
            expert(E // 2 - 1, 1, False, False, True)
            pe.wait_ge(s_y, E)
            y_rows().then_inc(s_yT_mm, 1)

            pe.wait_ge(s_row_idx, 1)
            with further_passes(pe):
                with pe.Fori(0, E * MORE) as n:
                    pe.wait_ge(o_sel, n + 1)
                    slot_tokens().then_inc(o_idx_mm, 1)
                    pe.wait_ge(o_xg, 16 * ST * (n + 1))
                    rows_transposed(0).then_inc(o_xT_mm, 1)
                    pe.wait_ge(o_x, n + 1)
                    pe.wait_ge(o_w, 48 * (n + 1))
                    for m in range(MT):
                        if m >= 4:
                            pe.wait_ge(o_hid, MT * n + m - 3)
                        for which in range(2):
                            for k in range(DT):
                                c0 = k * INNER + m * 128
                                last = pe.matmul(bank[:, m % 4, which * SLOTS:(which + 1) * SLOTS],
                                                 raw[:, 0, which, c0:c0 + 128], x_o[:, k, :], start=(k == 0), stop=(k == DT - 1))
                        last.then_inc(o_gu_mm, 1)
                    pe.wait_ge(o_hid, MT * n + MT)
                    for m in range(DT):
                        for t in range(MT):
                            last = pe.matmul(bank[:, 4, m * SLOTS:(m + 1) * SLOTS], w2_sb[:, 0, t, m * 128:(m + 1) * 128],
                                             hid[:, 0, t, :], start=(t == 0), stop=(t == MT - 1))
                    last.then_inc(o_y_mm, 1)
                    pe.wait_ge(o_y, n + 1)
                    y_rows().then_inc(o_yT_mm, 1)
                    pe.wait_ge(o_yr, n + 1)

        @block.scalar
        def _(act):
            act.dma_start(cst[:], consts).then_inc(s_small, 16)
            act.dma_start(vec[:], vecs).then_inc(s_small, 16)
            act.dma_start(gate_sb[:], gate).then_inc(s_bias, 16)
            act.dma_start(bv_rows[:], bv.partition_broadcast(GT)).then_inc(s_bias, 16)
            act.dma_start(bf_rows[:], bf.partition_broadcast(GT)).then_inc(s_bias, 16)

            def split_hi(par, j):
                act.activation(w_hi[:, par, j * WCH:(j + 1) * WCH],
                               raw[:, par].rearrange("p a c -> p (a c)")[:, j * WCH:(j + 1) * WCH], ACT.Copy).then_inc(s_whi, 1)

            for g in range(NG):
                n = GROUP[g]
                act.wait_ge(s_neg_top, g + 1)
                if g >= 2:
                    act.wait_ge(s_probT_mm, g - 1)
                act.activation(prob[0:n, g % 2, 0:n], score[0:n, g % 2, 0:n], ACT.Exp, bias=neg_top[0:n, g:g + 1],
                               accum_out=prob_sum[0:n, g:g + 1]).then_inc(s_prob, 1)
                if g == 0:
                    continue
                copies = [g - 1] + ([g] if g == NG - 1 else [])
                for c in copies:
                    n = GROUP[c]
                    act.wait_ge(s_probT_mm, c + 1)
                    if c >= 2:
                        act.wait_ge(s_attn_mm, c - 1)
                    act.activation(probT[0:n, c % 2, 0:n], bank[0:n, 4 + c % 2, 0:n], ACT.Copy).then_inc(s_probT, 1)
                    act.wait_ge(s_attn_mm, c + 1)
                    if c >= 2:
                        act.wait_ge(s_proj_mm, c - 1)
                    act.activation(attnT[:, c % 2, :, 0:n], bank[:, 6, 0:DT * 128].rearrange("p (m t) -> p m t", m=DT)[:, :, 0:n],
                                   ACT.Copy).then_inc(s_attn, 1)
            act.wait_ge(s_tri, 1)
            act.wait_ge(s_mv, NG)
            act.activation(std[:], mv[:, :, 1], ACT.Sqrt, bias=eps_col[:]).then_inc(s_std, 1)
            for j in range(NG // 2):
                act.wait_ge(s_h1T_mm, j + 1)
                for g in (2 * j, 2 * j + 1):
                    n = GROUP[g]
                    last = act.activation(h1T[:, g, :, 0:n],
                                          bank[:, j, (g % 2) * DT * 128:(g % 2 + 1) * DT * 128].rearrange("p (m t) -> p m t", m=DT)[:, :, 0:n],
                                          ACT.Copy)
                last.then_inc(s_h1T, 1)
            act.wait_ge(s_w1[0], 16)
            act.wait_ge(s_w3[0], 16)
            for j in range(MT):
                split_hi(0, j)

            def rows_out(i, par, again=True):
                e = 2 * i + par
                act.wait_ge(s_yT_mm, e + 1)
                if again:
                    act.wait_ge(s_y_dram[par], 16 * i)
                act.activation(y_sb[:, par].rearrange("p t d -> p (t d)"), bank[0:SLOT_T, 6, :], ACT.Copy).then_inc(s_yr, 1)

            def expert(i, par, split_next, prev, again):
                e = 2 * i + par
                for m in range(MT):
                    act.wait_ge(s_gu_mm, MT * e + m + 1)
                    if prev or m >= 2:
                        act.wait_ge(s_hid, MT * e + m - 1)
                    act.activation(gated[:, m % 2, :], bank[:, m % 4, 0:SLOTS], ACT.Silu).then_inc(s_silu, 1)
                    if split_next and m == 0:
                        act.wait_ge(s_w1[1 - par], 16 * (i + 1 + par))
                        act.wait_ge(s_w3[1 - par], 16 * (i + 1 + par))
                    if split_next and m < MT - 2:
                        split_hi(1 - par, m)
                    if prev and m == 2:
                        rows_out(i - 1 + par, 1 - par, again)
                if split_next:
                    for j in (MT - 2, MT - 1):
                        split_hi(1 - par, j)
                act.wait_ge(s_y_mm, e + 1)
                if prev:
                    act.wait_ge(s_yT_mm, e)
                act.activation(yT[:].rearrange("p m t -> p (m t)"), bank[:, 4, 0:DT * SLOTS], ACT.Copy).then_inc(s_y, 1)

            expert(0, 0, True, False, False)
            expert(0, 1, True, True, False)
            expert(1, 0, True, True, False)
            expert(1, 1, True, True, True)
            with act.Fori(2, E // 2 - 1) as i:
                for par in range(2):
                    expert(i, par, True, True, True)
            expert(E // 2 - 1, 0, True, True, True)
            expert(E // 2 - 1, 1, False, True, True)
            rows_out(E // 2 - 1, 1)
            act.wait_ge(s_gap, 1)
            act.activation(tanh_gap[:], gap[:], ACT.Tanh, scale=0.5).then_inc(s_tanh, 1)

            act.wait_ge(s_row_idx, 1)
            with further_passes(act):
                all_stored(act)
                with act.Fori(0, E * MORE) as n:
                    for m in range(MT):
                        act.wait_ge(o_gu_mm, MT * n + m + 1)
                        if m >= 2:
                            act.wait_ge(o_hid, MT * n + m - 1)
                        act.activation(gated[:, m % 2, :], bank[:, m % 4, 0:SLOTS], ACT.Silu).then_inc(o_silu, 1)
                    act.wait_ge(o_y_mm, n + 1)
                    act.activation(yT[:].rearrange("p m t -> p (m t)"), bank[:, 4, 0:DT * SLOTS], ACT.Copy).then_inc(o_y, 1)
                    act.wait_ge(o_yT_mm, n + 1)
                    act.activation(y_sb[:, 0].rearrange("p t d -> p (t d)"), bank[0:SLOT_T, 6, :], ACT.Copy).then_inc(o_yr, 1)
                    act.wait_ge(o_y_dram, 16 * (n + 1))

            act.wait_ge(s_mv2, NG)
            act.activation(std[:], mv[:, :, 1], ACT.Sqrt, bias=eps_col[:]).then_inc(s_std2, 1)

        @block.vector
        def _(dve):
            linked = [0]

            def link(ins):
                linked[0] += 1
                ins.then_inc(s_link, 1)
                dve.wait_ge(s_link, linked[0])

            dve.memset(eps_col[:], EPS).then_inc(s_tri, 1)
            dve.wait_ge(s_small, 32)
            pos_v = vec[:, V_POS:V_POS + DT * T].rearrange("p (m j) -> p m j", m=DT)
            dve.tensor_tensor(posb[:, :, 1:T], pos_v[:, :, 1:T],
                              vec[:, V_BT:V_BT + DT].unsqueeze(2).broadcast_to([128, DT, NP]), ALU.add)
            link(dve.tensor_tensor(posb[:, :, 0:1], pos_v[:, :, 0:1], vec[:, V_CLS:V_CLS + DT].unsqueeze(2), ALU.add))
            dve.tensor_copy(tri_b[:], cst[0:GT, C_TRI:C_TRI + GT])
            dve.tensor_copy(tid_b[:].rearrange("p g c -> p (g c)"), cst[0:GT, C_TID:C_TID + 2 * NG]).then_inc(s_tri, 1)
            dve.tensor_copy(hT[:].rearrange("p m (b j) -> p m b j", j=T)[:, :, :, 0],
                            posb[:, :, 0:1].broadcast_to([128, DT, B])).then_inc(s_hT, 1)
            for half in range(2):
                dve.wait_ge(s_patch_mm, half + 1)
                for m in range(DT):
                    dve.tensor_tensor(per_image(hT[:, m, half * HALF_T:(half + 1) * HALF_T], T)[:, :, 1:T],
                                      per_image(bank[:, 2 * half + m, 0:HALF_P], NP),
                                      posb[:, m, 1:T].unsqueeze(1).broadcast_to([128, HALF_B, NP]), ALU.add).then_inc(s_hT, 1)
            for half in range(2):
                for w in range(2):
                    n = 2 * half + w
                    dve.wait_ge(s_qk_mm, n + 1)
                    if n >= 2:
                        dve.wait_ge(s_rope, n - 1)
                    b0 = 4 * (1 - half) + 2 * w
                    for j, (eo, table) in enumerate(((0, cos8), (1, sin8), (1, cos8), (0, sin8))):
                        last = dve.scalar_tensor_tensor(out=per_image(rope_t[:, n % 2, j, :], T), in0=per_image(bank[:, b0 + eo, 0:HALF_T], T),
                                                        scalar=vec[:, (V_BQ, V_BK)[w] + eo:(V_BQ, V_BK)[w] + eo + 1],
                                                        in1=table, op0=ALU.add, op1=ALU.mult)
                    last.then_inc(s_rope_mul, 1)

            def group_in(g):
                n = GROUP[g]
                if g == 0:
                    dve.wait_ge(s_bias, 48)
                dve.wait_ge(s_vh_mm, g + 1)
                dve.tensor_tensor(v_sb[0:n, g, :], bank[0:n, g % 2, 0:D], bv_rows[0:n, :], ALU.add)
                dve.tensor_tensor(resid[0:n, g, :], bank[0:n, g % 2, D:2 * D], bf_rows[0:n, :], ALU.add).then_inc(s_vh, 1)
                dve.wait_ge(s_score_mm, g + 1)
                if g >= 2:
                    dve.wait_ge(s_prob, g - 1)
                dve.tensor_tensor_reduce(out=score[0:n, g % 2, 0:n], in0=bank[0:n, 2 + g % 2, 0:n], in1=mask[0:n, 0:n],
                                         scale=1.0 / np.sqrt(D), scalar=-3e38, op0=ALU.add, op1=ALU.max,
                                         accum_out=top[0:n, g:g + 1]).then_inc(s_score, 1)
                dve.wait_ge(s_score, g + 1)
                dve.tensor_scalar(neg_top[0:n, g:g + 1], top[0:n, g:g + 1], -1.0, None, ALU.mult).then_inc(s_neg_top, 1)

            group_in(0)
            group_in(1)
            dve.wait_ge(s_setup, 3)
            for g in range(NG):
                n = GROUP[g]
                if g + 2 < NG:
                    group_in(g + 2)
                dve.wait_ge(s_prob, g + 1)
                link(dve.reciprocal(prob_inv[0:n, g:g + 1], prob_sum[0:n, g:g + 1]))
                dve.wait_ge(s_proj_mm, g + 1)
                dve.scalar_tensor_tensor(out=pre[0:n, g, :], in0=bank[0:n, 7, 0:D], scalar=prob_inv[0:n, g:g + 1],
                                         in1=resid[0:n, g, :], op0=ALU.mult, op1=ALU.add).then_inc(s_pre, 1)
                dve.wait_ge(s_pre, g + 1)
                link(dve.bn_stats(stats[0:n, g, :], pre[0:n, g, :]))
                dve.bn_aggr(mv[0:n, g, :], stats[0:n, g, :]).then_inc(s_mv, 1)
            dve.wait_ge(s_std, 1)
            link(dve.reciprocal(rstd[:], std[:]))
            for g in range(NG):
                n = GROUP[g]
                dve.tensor_scalar(h1[0:n, g, :], pre[0:n, g, :], mv[0:n, g, 0:1], rstd[0:n, g:g + 1],
                                  ALU.subtract, ALU.mult).then_inc(s_h1, 1)

            dve.wait_ge(s_logit_mm, 1)
            full = NG - 1
            dve.tensor_copy(logit[:, 0:full, :], bank[0:GT, 3, 0:full * E].rearrange("p (g e) -> p g e", e=E))
            link(dve.tensor_copy(logit[0:GROUP[full], full, :], bank[0:GROUP[full], 3, full * E:NG * E]))
            shape4 = [GT, NG, E, E]
            other, own = logit[:].unsqueeze(2).broadcast_to(shape4), logit[:].unsqueeze(3).broadcast_to(shape4)
            dve.tensor_tensor(above[:], other, own, ALU.is_gt)
            link(dve.tensor_tensor(equal[:], other, own, ALU.is_equal))
            link(dve.tensor_tensor(equal[:], equal[:], lower.unsqueeze(1).broadcast_to(shape4), ALU.mult))
            link(dve.tensor_tensor(above[:], above[:], equal[:], ALU.add))
            link(dve.tensor_reduce(rank[:], above[:], AX_X, ALU.add))
            dve.tensor_scalar(picked_b[:], rank[:], 1.5, None, ALU.is_lt).then_inc(s_picked, 1)
            dve.tensor_scalar(picked[:], rank[:], 1.5, None, ALU.is_lt)
            dve.wait_ge(s_pos_mm, 1)
            link(dve.tensor_copy(pos[:], bank[0:GT, 4, 0:NG * E].rearrange("p (g e) -> p g e", e=E)))
            link(dve.scalar_tensor_tensor(out=pos1[:], in0=pos[:], scalar=1.0, in1=picked[:], op0=ALU.add, op1=ALU.mult))
            link(dve.tensor_scalar(slot_of[:].rearrange("p e g -> p g e"), pos1[:], -1.0, None, ALU.add))
            with whole_numbers():
                dve.reduce_max(most[0:1, 0:1], bank[0:1, 4, NG * E:(NG + 1) * E], AX_X).then_inc(s_pos, 1)

            def select(e, done):
                return dve.tensor_tensor(sel[:], iota.unsqueeze(1).broadcast_to([GT, NG, SLOTS]),
                                         slot_of[:, bass.ds(e, 1), :].rearrange("p o g -> p (o g)").unsqueeze(2).broadcast_to([GT, NG, SLOTS]),
                                         ALU.is_equal).then_inc(done, 1)

            def slot_index(par, done):
                numbers = bank[0:SLOT_T, 7, 0:2 * ST].rearrange("p (t c) -> p t c", c=2)
                with whole_numbers():
                    return dve.tensor_reduce(tok_idx[:, par, :, 0], numbers, AX_X, ALU.add).then_inc(done, 1)

            def split_rows(e, par):
                rows = bank[:, 5, 0:DT * SLOTS].rearrange("p (k t) -> p k t", k=DT)
                dve.wait_ge(s_xT_mm, e + 1)
                dve.tensor_copy(x_hi[:, par], rows).then_inc(s_xh, 1)
                dve.wait_ge(s_xh, e + 1)
                dve.tensor_tensor(x_lo[:, par], rows, x_hi[:, par].bitcast(F32), ALU.subtract).then_inc(s_x, 1)

            def split_lo(e, par, j):
                dve.wait_ge(s_whi, MT * e + j + 1)
                cs = slice(j * WCH, (j + 1) * WCH)
                dve.tensor_tensor(w_lo[:, par, cs], raw[:, par].rearrange("p a c -> p (a c)")[:, cs],
                                  w_hi[:, par, cs].bitcast(F32), ALU.subtract).then_inc(s_wlo, 1)

            for par in range(2):
                if par == 1:
                    dve.wait_ge(s_idx_mm, 1)
                select(par, s_sel)
                dve.wait_ge(s_idx_mm, par + 1)
                slot_index(par, s_idx)
            for j in range(MT):
                split_lo(0, 0, j)
            split_rows(0, 0)

            def expert(i, par, split_next, gather_next, next_rows):
                e = 2 * i + par
                for m in range(MT):
                    dve.wait_ge(s_silu, MT * e + m + 1)
                    dve.tensor_tensor(hid[:, par, m, :], gated[:, m % 2, :], bank[:, m % 4, SLOTS:2 * SLOTS],
                                      ALU.mult).then_inc(s_hid, 1)
                    if split_next and m < MT - 2:
                        split_lo(e + 1, 1 - par, m)
                    if gather_next and m == 1:
                        select(e + 2, s_sel)
                    if gather_next and m == 5:
                        dve.wait_ge(s_idx_mm, e + 3)
                        slot_index(par, s_idx)
                if next_rows:
                    split_rows(e + 1, 1 - par)
                if split_next:
                    for j in (MT - 2, MT - 1):
                        split_lo(e + 1, 1 - par, j)

            with dve.Fori(0, E // 2 - 1) as i:
                for par in range(2):
                    expert(i, par, True, True, True)

            dve.tensor_scalar(first[:], rank[:], 0.5, None, ALU.is_lt)
            link(dve.tensor_tensor(row_of[:], pos[:], row0.unsqueeze(1).broadcast_to([GT, NG, E]), ALU.add))
            for c in range(1, PASSES):
                link(dve.tensor_scalar(pos1[:], pos[:], float(c * SLOTS), float(PASS_ROWS - SLOTS), ALU.is_ge, ALU.mult))
                link(dve.tensor_tensor(row_of[:], row_of[:], pos1[:], ALU.add))
            link(dve.tensor_tensor(second[:], picked[:], first[:], ALU.subtract))
            for k, which in enumerate((first, second)):
                dve.tensor_tensor(pick_t[:, k], row_of[:], which[:], ALU.mult)
                link(dve.tensor_tensor(pick_t[:, 2 + k], logit[:], which[:], ALU.mult))
            for k in range(2):
                with whole_numbers():
                    dve.tensor_reduce(row_idx[:, k, :], pick_t[:, k], AX_X, ALU.add)
                last = dve.tensor_reduce((l1, l2)[k][:], pick_t[:, 2 + k], AX_X, ALU.add)
            link(last)
            dve.tensor_tensor(gap[:], l1[:], l2[:], ALU.subtract).then_inc(s_gap, 1)
            dve.tensor_scalar(most[0:1, 0:1], most[0:1, 0:1], 0.0, None, ALU.add).then_inc(s_row_idx, 1)

            expert(E // 2 - 1, 0, True, False, True)
            expert(E // 2 - 1, 1, False, False, False)

            with further_passes(dve):
                all_stored(dve)
                with dve.Fori(0, E) as e:
                    for c in range(MORE):
                        n = e * MORE + c
                        dve.tensor_scalar(pos1[:, :, 0], slot_of[:, bass.ds(e, 1), :].rearrange("p o g -> p (o g)"),
                                          -float(SLOTS * (c + 1)), None, ALU.add).then_inc(o_slot, 1)
                        dve.wait_ge(o_slot, n + 1)
                        dve.tensor_tensor(sel[:], iota.unsqueeze(1).broadcast_to([GT, NG, SLOTS]),
                                          pos1[:, :, 0:1].broadcast_to([GT, NG, SLOTS]), ALU.is_equal).then_inc(o_sel, 1)
                        dve.wait_ge(o_idx_mm, n + 1)
                        slot_index(0, o_idx)
                        dve.wait_ge(o_xT_mm, n + 1)
                        dve.tensor_copy(x_o, bank[:, 5, 0:DT * SLOTS].rearrange("p (k t) -> p k t", k=DT)).then_inc(o_x, 1)
                        for m in range(MT):
                            dve.wait_ge(o_silu, MT * n + m + 1)
                            dve.tensor_tensor(hid[:, 0, m, :], gated[:, m % 2, :], bank[:, m % 4, SLOTS:2 * SLOTS],
                                              ALU.mult).then_inc(o_hid, 1)
                        dve.wait_ge(o_yr, n + 1)

            dve.wait_ge(s_tanh, 1)
            dve.tensor_scalar(route_w[:, 0, :], tanh_gap[:], 0.5, 0.5, ALU.mult, ALU.add)
            link(dve.tensor_scalar(route_w[:, 1, :], tanh_gap[:], -0.5, 0.5, ALU.mult, ALU.add))
            for g in range(NG):
                n = GROUP[g]
                dve.wait_ge(s_y_tok[g], 32)
                link(dve.scalar_tensor_tensor(out=mix[0:n, g, :], in0=y_tok[0:n, 0, g, :], scalar=route_w[0:n, 0, g:g + 1],
                                              in1=h1[0:n, g, :], op0=ALU.mult, op1=ALU.add))
                link(dve.scalar_tensor_tensor(out=mix2[0:n, g, :], in0=y_tok[0:n, 1, g, :], scalar=route_w[0:n, 1, g:g + 1],
                                              in1=mix[0:n, g, :], op0=ALU.mult, op1=ALU.add))
                link(dve.bn_stats(stats[0:n, g, :], mix2[0:n, g, :]))
                dve.bn_aggr(mv[0:n, g, :], stats[0:n, g, :]).then_inc(s_mv2, 1)
            dve.wait_ge(s_std2, 1)
            link(dve.reciprocal(rstd[:], std[:]))
            for g in range(NG):
                n = GROUP[g]
                dve.tensor_scalar(out_sb[0:n, g, :], mix2[0:n, g, :], mv[0:n, g, 0:1], rstd[0:n, g:g + 1],
                                  ALU.subtract, ALU.mult).then_inc(s_out, 1)


def kernel(x, L0_tok_W, L0_tok_b, L0_tok_class_token, L0_tok_pos_embedding, L0_attn_Wq, L0_attn_bq, L0_attn_Wk,
           L0_attn_bk, L0_attn_Wv, L0_attn_bv, L0_attn_Wf, L0_attn_bf, L0_ffn_gate, L0_ffn_experts_w1,
           L0_ffn_experts_w2, L0_ffn_experts_w3):
    import concourse.bacc as bacc
    from concourse.bass_utils import run_bass_kernel_spmd

    def tiles(a):
        return a.reshape(-1, 128, a.shape[-1]).transpose(1, 0, 2)

    def columns(a):
        return np.asarray(a).reshape(DT, 128).T

    x = np.asarray(x)
    pt = x.reshape(B, CH, GRID, PATCH, GRID, PATCH).transpose(1, 3, 5, 0, 2, 4).reshape(KP // 2, 2, 128, 2, HALF_P)
    pt = pt.transpose(3, 0, 2, 1, 4)
    tw = np.asarray(L0_tok_W).T.reshape(KP // 2, 2, 128, D).transpose(0, 2, 1, 3)
    order = np.concatenate([np.arange(0, D, 2), np.arange(1, D, 2)])
    aw = np.stack([tiles(np.asarray(L0_attn_Wq)[order].T), tiles(np.asarray(L0_attn_Wk)[order].T),
                   tiles(np.asarray(L0_attn_Wv).T), tiles(np.asarray(L0_attn_Wf).T)], axis=1)
    pos = np.asarray(L0_tok_pos_embedding).reshape(T, DT, 128).transpose(2, 1, 0).reshape(128, DT * T)
    vecs = np.concatenate([columns(np.asarray(L0_attn_bq)[order]), columns(np.asarray(L0_attn_bk)[order]),
                           columns(L0_tok_b), columns(np.asarray(L0_tok_class_token).reshape(D)), pos], axis=1)

    def up(w):
        return np.asarray(w).reshape(E, DT, 128, INNER).transpose(0, 2, 1, 3).reshape(E, 128, DT * INNER)

    arrays = {
        "patches": pt, "tok_w": tw, "vecs": vecs, "attn_w": aw, "bv": np.asarray(L0_attn_bv), "bf": np.asarray(L0_attn_bf),
        "gate": tiles(np.asarray(L0_ffn_gate)), "w1": up(L0_ffn_experts_w1), "w3": up(L0_ffn_experts_w3),
        "w2": np.asarray(L0_ffn_experts_w2).reshape(E, MT, 128, D).transpose(0, 2, 1, 3), "consts": shape_constants(),
    }
    arrays = {k: np.ascontiguousarray(v) for k, v in arrays.items()}
    nc = bacc.Bacc("TRN2", target_bir_lowering=False, num_devices=1)
    args = [nc.dram_tensor(k, v.shape, mybir.dt.from_np(v.dtype), kind="ExternalInput").ap() for k, v in arrays.items()]
    out = nc.dram_tensor("out", (B, T, D), F32, kind="ExternalOutput").ap()
    vit_layer(nc, *args, out)
    r = run_bass_kernel_spmd(nc, [arrays], core_ids=[0])
    return r.results[0]["out"]
```

```python
from contextlib import ExitStack

import numpy as np

import concourse.bass as bass
from concourse import mybir

ALU = mybir.AluOpType
ACT = mybir.ActivationFunctionType
AX_X = mybir.AxisListType.X
F32 = mybir.dt.float32
BF16 = mybir.dt.bfloat16
U32 = mybir.dt.uint32
I32 = mybir.dt.int32

B, CH, IMG, PATCH = 16, 3, 96, 16
GRID = IMG // PATCH
NP = GRID * GRID
T = NP + 1
TOK = B * T
D = 256
DT = D // 128
KP = CH * PATCH * PATCH // 128
HALF_B = B // 2
HALF_P, HALF_T = HALF_B * NP, HALF_B * T
GB = 128 // T
GT = GB * T
NG = -(-B // GB)
GROUP = [min(GT, TOK - g * GT) for g in range(NG)]
E, INNER = 8, 1024
MT = INNER // 128
SLOTS = 208
ST = 2
SLOT_T = SLOTS // ST
PASSES = -(-TOK // SLOTS)
PASS_ROWS = E * SLOTS
LAST_ROW = 1 + (E - 1) * SLOTS
BATCHES = ((0, 4), (4, NG))
EPS = 1e-5
NEG = -1e30
REST = NG - 4 + 1
WIDTHS = (144, 160, 176, SLOTS)
WARM = 12

C_ID = 0
C_MASK = C_ID + 128
C_TRI = C_MASK + GT
C_COS = C_TRI + GT
C_SIN = C_COS + T
C_IOTA = C_SIN + T
C_ROW0 = C_IOTA + SLOTS
C_LT = C_ROW0 + E
C_TID = C_LT + E * E
C_W = C_TID + 2 * NG

V_BQ, V_BK, V_BT, V_CLS, V_BV, V_POS = 0, DT, 2 * DT, 3 * DT, 4 * DT, 5 * DT
V_W = V_POS + DT * T


def shape_constants():
    c = np.zeros((128, C_W), np.float32)
    c[:, C_ID:C_ID + 128] = np.eye(128)
    p, q = np.arange(GT)[:, None], np.arange(GT)[None, :]
    c[:GT, C_MASK:C_MASK + GT] = np.where((p // T == q // T) & (q <= p), 0.0, NEG)
    c[:GT, C_TRI:C_TRI + GT] = p < q
    freqs = (np.float32(1.0) / np.float32(10000.0) ** (np.arange(0, D, 2, dtype=np.float32) / np.float32(D)))
    ang = freqs.astype(np.float32)[:, None] * np.arange(T, dtype=np.float32)[None, :]
    c[:, C_COS:C_COS + T] = np.cos(ang)
    c[:, C_SIN:C_SIN + T] = np.sin(ang)
    c[:, C_IOTA:C_IOTA + SLOTS] = np.arange(SLOTS)
    c[:, C_ROW0:C_ROW0 + E] = 1 + np.arange(E) * SLOTS
    e, f = np.arange(E)[:, None], np.arange(E)[None, :]
    c[:, C_LT:C_LT + E * E] = (f < e).reshape(-1)
    for g in range(NG):
        token = g * GT + np.arange(128)
        c[:, C_TID + 2 * g] = token // 4 * 4
        c[:, C_TID + 2 * g + 1] = token % 4
    return c


def vit_layer(nc, patches, tok_w, vecs, attn_w, bf, gate, w1, w3, w2, consts, out):
    h1_dram = nc.dram_tensor("h1_rows", (TOK, D), F32, kind="Internal").ap()
    y_dram = nc.dram_tensor("expert_rows", (1 + PASSES * PASS_ROWS, D), F32, kind="Internal").ap()
    out_rows = out.rearrange("b j d -> (b j) d")

    with ExitStack() as ctx:
        def sb(name, shape, dt=F32):
            return ctx.enter_context(nc.sbuf_tensor(name, shape, dt))

        def sem(name):
            return ctx.enter_context(nc.semaphore(name))

        bank = ctx.enter_context(nc.psum_tensor("bank", [128, 8, 512], F32))

        cst = sb("cst", [128, C_W])
        vec = sb("vec", [128, V_W])
        bf_rows = sb("bf_rows", [GT, D])
        tok_w_sb = sb("tok_w_sb", [128, KP, D])
        patch_sb = sb("patch_sb", [128, 2, KP, HALF_P])
        attn_w_sb = sb("attn_w_sb", [128, 4, DT, D])
        gate_sb = sb("gate_sb", [128, DT, E])
        ident = cst[:, C_ID:C_ID + 128]
        mask = cst[0:GT, C_MASK:C_MASK + GT]
        iota = cst[0:GT, C_IOTA:C_IOTA + SLOTS]
        row0 = cst[0:GT, C_ROW0:C_ROW0 + E]
        lower = cst[0:GT, C_LT:C_LT + E * E].rearrange("p (e f) -> p e f", e=E)
        tri_b = sb("tri_b", [GT, GT], BF16)
        ones_b = sb("ones_b", [GT, GT], BF16)
        tid_b = sb("tid_b", [GT, NG, 2], BF16)
        ident_b = sb("ident_b", [GT, GT], BF16)
        warm_b = sb("warm_b", [128, 512], BF16)
        eps_col = sb("eps_col", [GT, 1])
        zero_row = sb("zero_row", [1, D])

        posb = sb("posb", [128, DT, T])
        bv_b = sb("bv_b", [128, DT, GT])
        bias_rows = sb("bias_rows", [GT, D])
        hT = sb("hT", [128, DT, TOK])
        rope_t = sb("rope_t", [128, 2, 4, HALF_T])
        qk = sb("qk", [128, 2, 2, TOK])
        v_sb = sb("v_sb", [GT, NG, D])
        resid = sb("resid", [GT, NG, D])
        score = sb("score", [GT, NG, GT])
        prob = sb("prob", [GT, NG, GT])
        probT = sb("probT", [GT, 2, GT])
        attnT = sb("attnT", [128, 2, DT, GT])
        top = sb("top", [GT, NG])
        neg_top = sb("neg_top", [GT, NG])
        prob_sum = sb("prob_sum", [GT, NG])
        prob_inv = sb("prob_inv", [GT, NG])
        pre = sb("pre", [GT, NG, D])
        stats = sb("stats", [GT, NG, 6])
        mv = sb("mv", [GT, NG, 2])
        std = sb("std", [GT, NG])
        rstd = sb("rstd", [GT, NG])
        h1 = sb("h1", [GT, NG, D])
        h1T = sb("h1T", [128, NG, DT, GT])

        logit = sb("logit", [GT, NG, E])
        above = sb("above", [GT, NG, E, E])
        equal = sb("equal", [GT, NG, E, E])
        rank = sb("rank", [GT, NG, E])
        picked = sb("picked", [GT, NG, E])
        picked_b = sb("picked_b", [GT, NG, E], BF16)
        first = sb("first", [GT, NG, E])
        second = sb("second", [GT, NG, E])
        pos1 = sb("pos1", [GT, NG, E])
        slot_of = sb("slot_of", [GT, NG, E])
        row_of = sb("row_of", [GT, NG, E])
        row_early = sb("row_early", [GT, NG, E])
        pick_t = sb("pick_t", [GT, 6, NG, E])
        row_idx = sb("row_idx", [GT, 2, NG], U32)
        early_idx = sb("early_idx", [GT, 2, NG], U32)
        count_f = sb("count_f", [1, E])
        count = sb("count", [1, E], I32)
        most = sb("most", [1, 1], I32)
        l1 = sb("l1", [GT, NG])
        l2 = sb("l2", [GT, NG])
        gap = sb("gap", [GT, NG])
        tanh_gap = sb("tanh_gap", [GT, NG])
        route_w = sb("route_w", [GT, 2, NG])
        last_w = sb("last_w", [GT, 3, NG])
        sel = sb("sel", [GT, 2, NG, SLOTS], BF16)
        selT = sb("selT", [SLOT_T, ST, NG, GT])
        tok_idx = sb("tok_idx", [SLOT_T, 2, ST, 1], U32)

        w13_sb = sb("w13_sb", [128, 2, 2, DT * INNER])
        w2_sb = sb("w2_sb", [128, 2, MT, D])
        xg = sb("xg", [SLOT_T, 2, ST, D])
        xT = sb("xT", [128, 2, DT, SLOTS])
        gated = sb("gated", [128, 2, SLOTS])
        hid = sb("hid", [128, MT, SLOTS])
        yT = sb("yT", [128, DT, SLOTS])
        y_sb = sb("y_sb", [SLOT_T, 2, ST, D])
        y_tok = sb("y_tok", [GT, 2, NG, D])
        mix = sb("mix", [GT, NG, D])
        mix2 = sb("mix2", [GT, NG, D])
        out_sb = pre

        s_front = [sem(f"s_front{k}") for k in range(KP // 2)]
        s_patch1 = sem("s_patch1")
        s_small = sem("s_small")
        s_attn_w = sem("s_attn_w")
        s_bias = sem("s_bias")
        s_w13 = [sem(f"s_w13_{p}") for p in range(2)]
        s_w2 = [sem(f"s_w2_{p}") for p in range(2)]
        s_zero_row = sem("s_zero_row")
        s_warm = sem("s_warm")
        s_setup = sem("s_setup")
        s_link = sem("s_link")
        s_const = sem("s_const")
        s_patch_mm = sem("s_patch_mm")
        s_hT = sem("s_hT")
        s_qk_mm = sem("s_qk_mm")
        s_rope_mul = sem("s_rope_mul")
        s_rope = sem("s_rope")
        s_v_mm = sem("s_v_mm")
        s_v = sem("s_v")
        s_cb_mm = sem("s_cb_mm")
        s_cb = sem("s_cb")
        s_score_mm = sem("s_score_mm")
        s_score = sem("s_score")
        s_neg_top = sem("s_neg_top")
        s_prob = sem("s_prob")
        s_row_mm = sem("s_row_mm")
        s_resid = sem("s_resid")
        s_probT_mm = sem("s_probT_mm")
        s_probT = sem("s_probT")
        s_attn_mm = sem("s_attn_mm")
        s_attn = sem("s_attn")
        s_proj_mm = sem("s_proj_mm")
        s_pre = sem("s_pre")
        s_mv = sem("s_mv")
        s_std = sem("s_std")
        s_h1 = sem("s_h1")
        s_h1_dram = sem("s_h1_dram")
        s_h1T_mm = sem("s_h1T_mm")
        s_h1T = sem("s_h1T")
        s_logit_mm = sem("s_logit_mm")
        s_picked = sem("s_picked")
        s_pos_mm = sem("s_pos_mm")
        s_slot = sem("s_slot")
        s_count = sem("s_count")
        s_rows = sem("s_rows")
        s_gap = sem("s_gap")
        s_tanh = sem("s_tanh")
        s_sel = sem("s_sel")
        s_idx_mm = sem("s_idx_mm")
        s_idx = sem("s_idx")
        s_gathers = sem("s_gathers")
        s_xg = [sem(f"s_xg{p}") for p in range(2)]
        s_xT_mm = sem("s_xT_mm")
        s_x = sem("s_x")
        s_gu_mm = sem("s_gu_mm")
        s_silu = sem("s_silu")
        s_hid = sem("s_hid")
        s_y_mm = sem("s_y_mm")
        s_y = sem("s_y")
        s_yT_mm = sem("s_yT_mm")
        s_yr = sem("s_yr")
        s_y_dram = [sem(f"s_y_dram{p}") for p in range(2)]
        s_selT_mm = sem("s_selT_mm")
        s_selT = sem("s_selT")
        s_y_tok = [sem(f"s_y_tok{g}") for g in range(NG)]
        s_mix = sem("s_mix")
        s_last_mm = sem("s_last_mm")
        s_mix2 = sem("s_mix2")
        s_mv2 = sem("s_mv2")
        s_std2 = sem("s_std2")
        s_out = sem("s_out")
        s_out_dram = sem("s_out_dram")
        o_w = sem("o_w")
        o_link = sem("o_link")
        o_slot = sem("o_slot")
        o_sel = sem("o_sel")
        o_idx_mm = sem("o_idx_mm")
        o_idx = sem("o_idx")
        o_xg = sem("o_xg")
        o_xT_mm = sem("o_xT_mm")
        o_x = sem("o_x")
        o_gu_mm = sem("o_gu_mm")
        o_silu = sem("o_silu")
        o_hid = sem("o_hid")
        o_y_mm = sem("o_y_mm")
        o_y = sem("o_y")
        o_yT_mm = sem("o_yT_mm")
        o_yr = sem("o_yr")
        o_y_dram = sem("o_y_dram")
        o_y_tok = sem("o_y_tok")

        cos8 = cst[:, C_COS:C_COS + T].unsqueeze(1).broadcast_to([128, HALF_B, T])
        sin8 = cst[:, C_SIN:C_SIN + T].unsqueeze(1).broadcast_to([128, HALF_B, T])

        def per_image(ap, n):
            return ap.rearrange("p (b j) -> p b j", j=n)

        def further_passes(eng):
            return eng.If(eng.value_load(most[0:1, 0:1], min_val=0, max_val=TOK) > SLOTS)

        def whole_numbers():
            return nc.allow_low_precision(reason="sums of whole numbers below 2**24, kept as integers")

        def all_stored(eng):
            for par in range(2):
                eng.wait_ge(s_y_dram[par], 16 * (E // 2))

        MORE = PASSES - 1
        LAST_PAIR = E // 2 - 1
        WF_BANK = (6, 2)

        block = ctx.enter_context(nc.Block())

        @block.sync
        def _(sp):
            for k in range(KP // 2):
                sp.dma_start(tok_w_sb[:, 2 * k:2 * k + 2, :], tok_w[k]).then_inc(s_front[k], 16)
                sp.dma_start(patch_sb[:, 0, 2 * k:2 * k + 2, :], patches[0, k]).then_inc(s_front[k], 16)
            for k in range(KP // 2):
                sp.dma_start(patch_sb[:, 1, 2 * k:2 * k + 2, :], patches[1, k]).then_inc(s_patch1, 16)
            sp.dma_start(attn_w_sb[:], attn_w).then_inc(s_attn_w, 16)

            def load_w13(e, par):
                sp.dma_start(w13_sb[:, par, 0, :], w1[bass.ds(e, 1)].rearrange("o p c -> (o p) c")).then_inc(s_w13[par], 16)
                sp.dma_start(w13_sb[:, par, 1, :], w3[bass.ds(e, 1)].rearrange("o p c -> (o p) c")).then_inc(s_w13[par], 16)

            def load_w2(e, par):
                sp.dma_start(w2_sb[:, par], w2[bass.ds(e, 1)].rearrange("o p m d -> (o p) m d")).then_inc(s_w2[par], 16)

            for par in range(2):
                load_w13(par, par)
                load_w2(par, par)
            sp.wait_ge(s_setup, 4)
            sp.dma_start(y_dram[0:1, :], zero_row[:]).then_inc(s_zero_row, 16)
            for g in range(NG):
                sp.wait_ge(s_h1, g + 1)
                sp.dma_start(h1_dram[g * GT:g * GT + GROUP[g], :], h1[0:GROUP[g], g, :]).then_inc(s_h1_dram, 16)

            def expert(i, par, load):
                e = 2 * i + par
                row = sp.snap(e * SLOTS + 1)
                if load:
                    sp.wait_ge(s_gu_mm, MT * e + MT)
                    load_w13(e + 2, par)
                    sp.wait_ge(s_y_mm, e + 1)
                    load_w2(e + 2, par)
                sp.wait_ge(s_yr, e + 1)
                sp.dma_start(y_dram[bass.ds(row, SLOTS), :].rearrange("(t p) d -> p t d", p=SLOT_T),
                             y_sb[:, par]).then_inc(s_y_dram[par], 16)

            with sp.Fori(0, LAST_PAIR) as i:
                for par in range(2):
                    expert(i, par, True)
            for par in range(2):
                expert(LAST_PAIR, par, False)

            sp.wait_ge(s_count, 1)
            with further_passes(sp):
                with sp.Fori(0, E) as e:
                    for c in range(MORE):
                        n = e * MORE + c
                        all_stored(sp)
                        sp.dma_start(w13_sb[:, 0, 0, :], w1[bass.ds(e, 1)].rearrange("o p c -> (o p) c")).then_inc(o_w, 16)
                        sp.dma_start(w13_sb[:, 0, 1, :], w3[bass.ds(e, 1)].rearrange("o p c -> (o p) c")).then_inc(o_w, 16)
                        sp.dma_start(w2_sb[:, 0], w2[bass.ds(e, 1)].rearrange("o p m d -> (o p) m d")).then_inc(o_w, 16)
                        row = sp.snap(e * SLOTS + (1 + (c + 1) * PASS_ROWS))
                        sp.wait_ge(o_yr, n + 1)
                        sp.dma_start(y_dram[bass.ds(row, SLOTS), :].rearrange("(t p) d -> p t d", p=SLOT_T),
                                     y_sb[:, 0]).then_inc(o_y_dram, 16)
                sp.wait_ge(o_y_dram, 16 * E * MORE)
            for g in range(NG):
                sp.wait_ge(s_out, g + 1)
                sp.dma_start(out_rows[g * GT:g * GT + GROUP[g], :], out_sb[0:GROUP[g], g, :]).then_inc(s_out_dram, 16)
            sp.wait_ge(s_out_dram, 16 * NG)
            sp.wait_ge(s_h1_dram, 16 * NG)
            sp.wait_ge(s_zero_row, 16)
            all_stored(sp)

        @block.gpsimd
        def _(pool):
            pool.memset(ones_b[:], 1.0).then_inc(s_setup, 1)
            pool.memset(logit[:], 0.0).then_inc(s_setup, 1)
            pool.memset(y_sb[:], 0.0).then_inc(s_setup, 1)
            pool.memset(zero_row[:], 0.0).then_inc(s_setup, 1)
            for half in range(2):
                for w in range(2):
                    n = 2 * half + w
                    cols = slice(half * HALF_T, (half + 1) * HALF_T)
                    pool.wait_ge(s_rope_mul, n + 1)
                    pool.tensor_tensor(qk[:, w, 0, cols], rope_t[:, n % 2, 0, :], rope_t[:, n % 2, 1, :], ALU.subtract)
                    pool.tensor_tensor(qk[:, w, 1, cols], rope_t[:, n % 2, 2, :], rope_t[:, n % 2, 3, :],
                                       ALU.add).then_inc(s_rope, 1)

            def gather(e, par):
                pool.wait_ge(s_idx, e + 1)
                pool.sem_inc(s_gathers, 1)
                for t in range(ST):
                    pool.indirect_dma_start(xg[:, par, t, :], None, h1_dram[:, :],
                                            bass.IndirectOffsetOnAxis(tok_idx[:, par, t, :], 0)).then_inc(s_xg[par], 16)

            pool.wait_ge(s_h1_dram, 16 * NG)
            for par in range(2):
                gather(par, par)
            with pool.Fori(0, LAST_PAIR) as i:
                for par in range(2):
                    e = 2 * i + par
                    gather(e + 2, par)

            def token_rows(idx, rows, done):
                for g in range(NG):
                    for k in range(2):
                        pool.indirect_dma_start(y_tok[0:GROUP[g], k, g, :], None, y_dram[0:rows, :],
                                                bass.IndirectOffsetOnAxis(idx[0:GROUP[g], k, g:g + 1], 0)).then_inc(done(g), 16)

            pool.wait_ge(s_rows, 1)
            pool.wait_ge(s_zero_row, 16)
            pool.wait_ge(s_y_dram[0], 16 * (E // 2))
            pool.wait_ge(s_y_dram[1], 16 * (E // 2 - 1))
            token_rows(early_idx, LAST_ROW, lambda g: s_y_tok[g])

            with further_passes(pool):
                all_stored(pool)
                with pool.Fori(0, E * MORE) as n:
                    pool.wait_ge(o_idx, n + 1)
                    pool.sem_inc(s_gathers, 1)
                    for t in range(ST):
                        pool.indirect_dma_start(xg[:, 0, t, :], None, h1_dram[:, :],
                                                bass.IndirectOffsetOnAxis(tok_idx[:, 0, t, :], 0)).then_inc(o_xg, 16)
                pool.wait_ge(o_y_dram, 16 * E * MORE)
                pool.wait_ge(s_mix, NG)
                token_rows(row_idx, 1 + PASSES * PASS_ROWS, lambda g: o_y_tok)

        @block.tensor
        def _(pe):
            def keep_warm(n, banks):
                for k in range(n):
                    pe.matmul(bank[:, banks[k % len(banks)], :], warm_b[:, 0:128], warm_b[:], start=True, stop=True)

            pe.wait_ge(s_warm, 1)
            keep_warm(WARM, (7,))
            for half in range(2):
                for k in range(KP):
                    if half == 0 and k % 2 == 0:
                        pe.wait_ge(s_front[k // 2], 32)
                    if half == 1 and k == 0:
                        pe.wait_ge(s_patch1, 16 * (KP // 2))
                    for m in range(DT):
                        last = pe.matmul(bank[:, 2 * half + m, 0:HALF_P], tok_w_sb[:, k, m * 128:(m + 1) * 128],
                                         patch_sb[:, half, k, :], start=(k == 0), stop=(k == KP - 1))
                last.then_inc(s_patch_mm, 1)
            pe.wait_ge(s_attn_w, 16)
            for half in range(2):
                pe.wait_ge(s_hT, 1 + DT * (half + 1))
                for w in range(2):
                    for eo in range(2):
                        for k in range(DT):
                            last = pe.matmul(bank[:, 4 * (1 - half) + 2 * w + eo, 0:HALF_T],
                                             attn_w_sb[:, w, k, eo * 128:(eo + 1) * 128],
                                             hT[:, k, half * HALF_T:(half + 1) * HALF_T], start=(k == 0), stop=(k == DT - 1))
                    last.then_inc(s_qk_mm, 1)

            def cols(g):
                return slice(g * GT, g * GT + GROUP[g])

            def values(j):
                for g in (2 * j, 2 * j + 1):
                    n = GROUP[g]
                    for k in range(DT):
                        last = pe.matmul(bank[0:n, 4 + j, (g % 2) * D:(g % 2 + 1) * D], hT[:, k, cols(g)], attn_w_sb[:, 2, k, :],
                                         start=(k == 0), stop=(k == DT - 1))
                last.then_inc(s_v_mm, 1)

            def scores(j):
                for g in (2 * j, 2 * j + 1):
                    n = GROUP[g]
                    for eo in range(2):
                        last = pe.matmul(bank[0:n, (7, 0, 1)[j], (g % 2) * 128:(g % 2) * 128 + n], qk[:, 0, eo, cols(g)],
                                         qk[:, 1, eo, cols(g)], start=(eo == 0), stop=(eo == 1))
                last.then_inc(s_score_mm, 1)

            def token_rows(j):
                for g in (2 * j, 2 * j + 1):
                    n = GROUP[g]
                    for k in range(DT):
                        last = pe.transpose(bank[0:n, (2, 3, 7)[j], (g % 2 * DT + k) * 128:(g % 2 * DT + k + 1) * 128],
                                            hT[:, k, cols(g)], ident)
                last.then_inc(s_row_mm, 1)

            pe.wait_ge(s_rope_mul, 2)
            values(0)
            pe.wait_ge(s_rope, 2)
            scores(0)
            values(1)
            values(2)
            pe.wait_ge(s_const, 4)
            pe.wait_ge(s_v, 1)
            for k in range(DT):
                last = pe.matmul(bank[0:GT, 4, 0:D], bv_b[:, k, :], attn_w_sb[:, 3, k, :], start=(k == 0), stop=(k == DT - 1))
            last.then_inc(s_cb_mm, 1)
            pe.wait_ge(s_rope_mul, 4)
            token_rows(0)
            pe.wait_ge(s_rope, 4)
            scores(1)
            scores(2)
            token_rows(1)
            pe.wait_ge(s_score, 2)
            token_rows(2)

            def probs_transposed(g):
                n = GROUP[g]
                pe.wait_ge(s_prob, max(g + 1, 4))
                if g >= 1:
                    pe.wait_ge(s_probT, g)
                pe.transpose(bank[0:n, 0, 0:n], prob[0:n, g, 0:n], cst[0:n, C_ID:C_ID + n]).then_inc(s_probT_mm, 1)

            def attention(g):
                n = GROUP[g]
                pe.wait_ge(s_probT, g + 1)
                pe.wait_ge(s_v, g // 2 + 1)
                if g == 0:
                    pe.wait_ge(s_cb, 1)
                else:
                    pe.wait_ge(s_attn, g)
                for m in range(DT):
                    last = pe.matmul(bank[:, 4, m * 128:m * 128 + n], v_sb[0:n, g, m * 128:(m + 1) * 128],
                                     probT[0:n, g % 2, 0:n], start=True, stop=True)
                last.then_inc(s_attn_mm, 1)

            def projection(g):
                n = GROUP[g]
                pe.wait_ge(s_attn, g + 1)
                if g == 0:
                    pe.wait_ge(s_v, 3)
                elif g == 1:
                    pe.wait_ge(s_resid, 2)
                else:
                    pe.wait_ge(s_pre, g - 1)
                for k in range(DT):
                    last = pe.matmul(bank[0:n, WF_BANK[g % 2], 0:D], attnT[:, g % 2, k, 0:n], attn_w_sb[:, 3, k, :],
                                     start=(k == 0), stop=(k == DT - 1))
                last.then_inc(s_proj_mm, 1)

            def h1_transposed(g):
                n = GROUP[g]
                pe.wait_ge(s_h1, g + 1)
                if g == 0:
                    pe.wait_ge(s_resid, 4)
                else:
                    pe.wait_ge(s_h1T, g)
                for k in range(DT):
                    last = pe.transpose(bank[:, 3, k * 128:k * 128 + n], h1[0:n, g, k * 128:(k + 1) * 128], cst[0:n, C_ID:C_ID + n])
                last.then_inc(s_h1T_mm, 1)

            def logits(g):
                b = 0 if g < BATCHES[1][0] else 1
                n, c = GROUP[g], g - BATCHES[b][0]
                pe.wait_ge(s_h1T, g + 1)
                for k in range(DT):
                    last = pe.matmul(bank[0:n, (5, 1)[b], c * E:(c + 1) * E], h1T[:, g, k, 0:n], gate_sb[:, k, :],
                                     start=(k == 0), stop=(k == DT - 1))
                if g + 1 == BATCHES[b][1]:
                    last.then_inc(s_logit_mm, 1)

            def ahead_first():
                g1 = BATCHES[0][1]
                pe.wait_ge(s_picked, 1)
                pe.wait_ge(s_resid, 6)
                for g in range(g1):
                    for j in range(g):
                        pe.matmul(bank[0:GT, 7, g * E:(g + 1) * E], ones_b[:], picked_b[:, j, :], start=(j == 0), stop=False)
                    last = pe.matmul(bank[0:GT, 7, g * E:(g + 1) * E], tri_b[:], picked_b[:, g, :], start=(g == 0), stop=True)
                last.then_inc(s_pos_mm, 1)
                pe.wait_ge(s_probT, NG)
                for j in range(g1):
                    pe.matmul(bank[0:GT, 0, 0:REST * E].rearrange("p (r e) -> p r e", e=E), ones_b[:],
                              picked_b[:, j:j + 1, :].broadcast_to([GT, REST, E]), start=(j == 0), stop=False)

            def ahead_second():
                g1 = BATCHES[1][0]
                pe.wait_ge(s_picked, 2)
                for g in range(g1, NG):
                    n, c = GROUP[g], g - g1
                    pe.matmul(bank[0:GT, 0, (c + 1) * E:REST * E].rearrange("p (r e) -> p r e", e=E), ones_b[0:n, :],
                              picked_b[0:n, g:g + 1, :].broadcast_to([n, REST - c - 1, E]), start=False, stop=False)
                    last = pe.matmul(bank[0:GT, 0, c * E:(c + 1) * E], tri_b[0:n, :], picked_b[0:n, g, :], start=False, stop=(g == NG - 1))
                last.then_inc(s_pos_mm, 1)

            probs_transposed(0)
            probs_transposed(1)
            attention(0)
            pe.wait_ge(s_bias, 32)
            for g in range(NG):
                if g + 2 < NG:
                    probs_transposed(g + 2)
                if g + 1 < NG:
                    attention(g + 1)
                projection(g)
                if g >= 2:
                    h1_transposed(g - 2)
                if g >= 3:
                    logits(g - 3)
            h1_transposed(NG - 2)
            logits(NG - 3)
            h1_transposed(NG - 1)
            logits(NG - 2)
            ahead_first()
            logits(NG - 1)
            ahead_second()

            def slot_tokens(par):
                for t in range(ST):
                    for g in range(NG):
                        n = GROUP[g]
                        last = pe.matmul(bank[0:SLOT_T, 7, 2 * t:2 * t + 2], sel[0:n, par, g, t * SLOT_T:(t + 1) * SLOT_T],
                                         tid_b[0:n, g, :], start=(g == 0), stop=(g == NG - 1))
                return last

            def rows_transposed(par):
                for k in range(DT):
                    for t in range(ST):
                        last = pe.transpose(bank[:, 5, (k * ST + t) * SLOT_T:(k * ST + t + 1) * SLOT_T],
                                            xg[:, par, t, k * 128:(k + 1) * 128], cst[0:SLOT_T, C_ID:C_ID + SLOT_T])
                return last

            def y_rows():
                for t in range(ST):
                    for m in range(DT):
                        last = pe.transpose(bank[0:SLOT_T, 6, (t * DT + m) * 128:(t * DT + m + 1) * 128],
                                            yT[:, m, t * SLOT_T:(t + 1) * SLOT_T], ident)
                return last

            def gate_up(par, m, x, width):
                for which in range(2):
                    for k in range(DT):
                        c0 = k * INNER + m * 128
                        last = pe.matmul(bank[:, m % 4, which * SLOTS:which * SLOTS + width], w13_sb[:, par, which, c0:c0 + 128],
                                         x[:, k, 0:width], start=(k == 0), stop=(k == DT - 1))
                return last

            for par in range(2):
                pe.wait_ge(s_sel, par + 1)
                pe.wait_ge(s_slot, 2) if par == 0 else pe.wait_ge(s_idx, 1)
                slot_tokens(par).then_inc(s_idx_mm, 1)
            pe.wait_ge(s_count, 1)
            keep_warm(WARM, tuple(range(5)))
            pe.wait_ge(s_xg[0], 16 * ST)
            rows_transposed(0).then_inc(s_xT_mm, 1)

            def products(i, par, next_rows, prev, width):
                e = 2 * i + par
                for m in range(MT):
                    if m >= 4 or prev:
                        pe.wait_ge(s_hid, MT * e + m - 3)
                    gate_up(par, m, xT[:, par], width).then_inc(s_gu_mm, 1)
                if next_rows:
                    pe.wait_ge(s_xg[1 - par], 16 * ST * (i + 1 + par))
                    rows_transposed(1 - par).then_inc(s_xT_mm, 1)
                else:
                    for t in range(ST):
                        for g in range(NG):
                            n = GROUP[g]
                            last = pe.transpose(bank[0:SLOT_T, (5, 7)[t], :].bitcast(BF16)[:, g * 128:g * 128 + n],
                                                sel[0:n, par, g, t * SLOT_T:(t + 1) * SLOT_T], ident_b[0:n, 0:n])
                    last.then_inc(s_selT_mm, 1)
                pe.wait_ge(s_w2[par], 16 * (i + 1))
                for m in range(DT):
                    for t in range(MT):
                        if m == 0:
                            pe.wait_ge(s_hid, MT * e + t + 1)
                        last = pe.matmul(bank[:, 4, m * SLOTS:m * SLOTS + width], w2_sb[:, par, t, m * 128:(m + 1) * 128],
                                         hid[:, t, 0:width], start=(t == 0), stop=(t == MT - 1))
                last.then_inc(s_y_mm, 1)

            def narrowest(tokens, widths, work):
                if len(widths) == 1:
                    work(widths[0])
                else:
                    with pe.If(tokens > widths[0]):
                        narrowest(tokens, widths[1:], work)
                    with pe.Else():
                        work(widths[0])

            def expert(i, par, gather_next, next_rows, prev):
                e = 2 * i + par
                tokens = pe.value_load(count[0:1, bass.ds(e, 1)], min_val=0, max_val=TOK)
                pe.wait_ge(s_x, e + 1)
                pe.wait_ge(s_w13[par], 32 * (i + 1))
                narrowest(tokens, WIDTHS if next_rows else WIDTHS[-1:], lambda width: products(i, par, next_rows, prev, width))
                if gather_next:
                    pe.wait_ge(s_sel, e + 3)
                    slot_tokens(par).then_inc(s_idx_mm, 1)
                pe.wait_ge(s_y, e + 1)
                if prev:
                    pe.wait_ge(s_yr, e)
                y_rows().then_inc(s_yT_mm, 1)

            expert(0, 0, True, True, False)
            expert(0, 1, True, True, True)
            with pe.Fori(1, LAST_PAIR) as i:
                for par in range(2):
                    expert(i, par, True, True, True)
            expert(LAST_PAIR, 0, False, True, True)
            expert(LAST_PAIR, 1, False, False, True)

            with further_passes(pe):
                with pe.Fori(0, E * MORE) as n:
                    pe.wait_ge(o_sel, n + 1)
                    slot_tokens(0).then_inc(o_idx_mm, 1)
                    pe.wait_ge(o_xg, 16 * ST * (n + 1))
                    rows_transposed(0).then_inc(o_xT_mm, 1)
                    pe.wait_ge(o_x, n + 1)
                    pe.wait_ge(o_w, 48 * (n + 1))
                    for m in range(MT):
                        if m >= 4:
                            pe.wait_ge(o_hid, MT * n + m - 3)
                        gate_up(0, m, xT[:, 0], SLOTS).then_inc(o_gu_mm, 1)
                    pe.wait_ge(o_hid, MT * n + MT)
                    for m in range(DT):
                        for t in range(MT):
                            last = pe.matmul(bank[:, 4, m * SLOTS:(m + 1) * SLOTS], w2_sb[:, 0, t, m * 128:(m + 1) * 128],
                                             hid[:, t, :], start=(t == 0), stop=(t == MT - 1))
                    last.then_inc(o_y_mm, 1)
                    pe.wait_ge(o_y, n + 1)
                    y_rows().then_inc(o_yT_mm, 1)
                    pe.wait_ge(o_yr, n + 1)

            pe.wait_ge(s_yr, E)
            pe.wait_ge(s_selT, 1)
            for g in range(NG):
                n = GROUP[g]
                if g >= 4:
                    pe.wait_ge(s_mix2, g - 3)
                for t in range(ST):
                    last = pe.matmul(bank[0:n, g % 4, 0:D], selT[:, t, g, 0:n], y_sb[:, 1, t, :], start=(t == 0), stop=(t == ST - 1))
                last.then_inc(s_last_mm, 1)

        @block.scalar
        def _(act):
            act.dma_start(cst[:], consts).then_inc(s_small, 16)
            act.dma_start(vec[:], vecs).then_inc(s_small, 16)
            act.dma_start(gate_sb[:], gate).then_inc(s_bias, 16)
            act.dma_start(bf_rows[:], bf.partition_broadcast(GT)).then_inc(s_bias, 16)

            def load_table(func):
                act.activation(std[0:1, 0:1], eps_col[0:1, :], func)

            def values_in(j):
                act.wait_ge(s_v_mm, j + 1)
                for g in (2 * j, 2 * j + 1):
                    n = GROUP[g]
                    last = act.activation(v_sb[0:n, g, :], bank[0:n, 4 + j, (g % 2) * D:(g % 2 + 1) * D], ACT.Copy)
                last.then_inc(s_v, 1)

            def probs(g):
                n = GROUP[g]
                act.wait_ge(s_neg_top, g + 1)
                act.activation(prob[0:n, g, 0:n], score[0:n, g, 0:n], ACT.Exp, bias=neg_top[0:n, g:g + 1],
                               accum_out=prob_sum[0:n, g:g + 1]).then_inc(s_prob, 1)

            def probT_in(g):
                n = GROUP[g]
                act.wait_ge(s_probT_mm, g + 1)
                if g >= 2:
                    act.wait_ge(s_attn_mm, g - 1)
                act.activation(probT[0:n, g % 2, 0:n], bank[0:n, 0, 0:n], ACT.Copy).then_inc(s_probT, 1)

            def attn_in(g):
                n = GROUP[g]
                act.wait_ge(s_attn_mm, g + 1)
                if g >= 2:
                    act.wait_ge(s_proj_mm, g - 1)
                act.activation(attnT[:, g % 2, :, 0:n], bank[:, 4, 0:DT * 128].rearrange("p (m t) -> p m t", m=DT)[:, :, 0:n],
                               ACT.Copy).then_inc(s_attn, 1)

            def root(g):
                n = GROUP[g]
                act.wait_ge(s_mv, g + 1)
                act.activation(std[0:n, g:g + 1], mv[0:n, g, 1:2], ACT.Sqrt, bias=eps_col[0:n, :]).then_inc(s_std, 1)

            def h1T_in(g):
                n = GROUP[g]
                act.wait_ge(s_h1T_mm, g + 1)
                act.activation(h1T[:, g, :, 0:n], bank[:, 3, 0:DT * 128].rearrange("p (m t) -> p m t", m=DT)[:, :, 0:n],
                               ACT.Copy).then_inc(s_h1T, 1)

            act.wait_ge(s_const, 1)
            load_table(ACT.Exp)
            values_in(0)
            probs(0)
            probs(1)
            values_in(1)
            values_in(2)
            for g in range(2, NG):
                probs(g)
            load_table(ACT.Sqrt)
            probT_in(0)
            probT_in(1)
            attn_in(0)
            for g in range(NG):
                if g + 2 < NG:
                    probT_in(g + 2)
                if g + 1 < NG:
                    attn_in(g + 1)
                if g >= 1:
                    root(g - 1)
                if g >= 2:
                    h1T_in(g - 2)
            root(NG - 1)
            h1T_in(NG - 2)
            h1T_in(NG - 1)
            act.wait_ge(s_std, NG)
            load_table(ACT.Silu)

            def expert(i, par, prev):
                e = 2 * i + par
                for m in range(MT):
                    act.wait_ge(s_gu_mm, MT * e + m + 1)
                    if prev or m >= 2:
                        act.wait_ge(s_hid, MT * e + m - 1)
                    act.activation(gated[:, m % 2, :], bank[:, m % 4, 0:SLOTS], ACT.Silu).then_inc(s_silu, 1)

            def y_in(i, par, again):
                e = 2 * i + par
                act.wait_ge(s_y_mm, e + 1)
                act.activation(yT[:].rearrange("p m t -> p (m t)"), bank[:, 4, 0:DT * SLOTS], ACT.Copy).then_inc(s_y, 1)
                act.wait_ge(s_yT_mm, e + 1)
                if again:
                    act.wait_ge(s_y_dram[par], 16 * i)
                act.activation(y_sb[:, par].rearrange("p t d -> p (t d)"), bank[0:SLOT_T, 6, :], ACT.Copy).then_inc(s_yr, 1)

            expert(0, 0, False)
            act.wait_ge(s_setup, 4)
            y_in(0, 0, False)
            expert(0, 1, True)
            y_in(0, 1, False)
            with act.Fori(1, LAST_PAIR) as i:
                for par in range(2):
                    expert(i, par, True)
                    y_in(i, par, True)
            expert(LAST_PAIR, 0, True)
            y_in(LAST_PAIR, 0, True)
            act.wait_ge(s_gap, 1)
            act.activation(tanh_gap[:], gap[:], ACT.Tanh, scale=0.5).then_inc(s_tanh, 1)
            expert(LAST_PAIR, 1, True)
            load_table(ACT.Sqrt)
            act.wait_ge(s_selT_mm, 1)
            for t in range(ST):
                for g0, g1, n in ((0, NG - 1, GT), (NG - 1, NG, GROUP[NG - 1])):
                    last = act.activation(selT[:, t, g0:g1, 0:n],
                                          bank[0:SLOT_T, (5, 7)[t], :].bitcast(BF16)[:, g0 * 128:g1 * 128].rearrange("p (g c) -> p g c", c=128)[:, :, 0:n],
                                          ACT.Copy)
            last.then_inc(s_selT, 1)
            y_in(LAST_PAIR, 1, True)

            with further_passes(act):
                all_stored(act)
                with act.Fori(0, E * MORE) as n:
                    for m in range(MT):
                        act.wait_ge(o_gu_mm, MT * n + m + 1)
                        if m >= 2:
                            act.wait_ge(o_hid, MT * n + m - 1)
                        act.activation(gated[:, m % 2, :], bank[:, m % 4, 0:SLOTS], ACT.Silu).then_inc(o_silu, 1)
                    act.wait_ge(o_y_mm, n + 1)
                    act.activation(yT[:].rearrange("p m t -> p (m t)"), bank[:, 4, 0:DT * SLOTS], ACT.Copy).then_inc(o_y, 1)
                    act.wait_ge(o_yT_mm, n + 1)
                    act.activation(y_sb[:, 0].rearrange("p t d -> p (t d)"), bank[0:SLOT_T, 6, :], ACT.Copy).then_inc(o_yr, 1)
                    act.wait_ge(o_y_dram, 16 * (n + 1))

            for g in range(NG):
                n = GROUP[g]
                act.wait_ge(s_mv2, g + 1)
                act.activation(std[0:n, g:g + 1], mv[0:n, g, 1:2], ACT.Sqrt, bias=eps_col[0:n, :]).then_inc(s_std2, 1)

        @block.vector
        def _(dve):
            linked = {s_link: 0, o_link: 0}

            def link(ins, done=s_link):
                linked[done] += 1
                ins.then_inc(done, 1)
                dve.wait_ge(done, linked[done])

            dve.memset(warm_b[:], 0.0).then_inc(s_warm, 1)
            dve.memset(eps_col[:], EPS).then_inc(s_const, 1)
            dve.wait_ge(s_small, 32)
            pos_v = vec[:, V_POS:V_POS + DT * T].rearrange("p (m j) -> p m j", m=DT)
            dve.tensor_tensor(posb[:, :, 1:T], pos_v[:, :, 1:T],
                              vec[:, V_BT:V_BT + DT].unsqueeze(2).broadcast_to([128, DT, NP]), ALU.add)
            link(dve.tensor_tensor(posb[:, :, 0:1], pos_v[:, :, 0:1], vec[:, V_CLS:V_CLS + DT].unsqueeze(2), ALU.add))
            dve.tensor_copy(tri_b[:], cst[0:GT, C_TRI:C_TRI + GT]).then_inc(s_const, 1)
            dve.tensor_copy(ident_b[:], cst[0:GT, C_ID:C_ID + GT]).then_inc(s_const, 1)
            dve.tensor_copy(tid_b[:].rearrange("p g c -> p (g c)"), cst[0:GT, C_TID:C_TID + 2 * NG])
            dve.tensor_copy(bv_b[:], vec[:, V_BV:V_BV + DT].unsqueeze(2).broadcast_to([128, DT, GT])).then_inc(s_const, 1)
            dve.tensor_copy(hT[:].rearrange("p m (b j) -> p m b j", j=T)[:, :, :, 0],
                            posb[:, :, 0:1].broadcast_to([128, DT, B])).then_inc(s_hT, 1)
            for half in range(2):
                dve.wait_ge(s_patch_mm, half + 1)
                for m in range(DT):
                    dve.tensor_tensor(per_image(hT[:, m, half * HALF_T:(half + 1) * HALF_T], T)[:, :, 1:T],
                                      per_image(bank[:, 2 * half + m, 0:HALF_P], NP),
                                      posb[:, m, 1:T].unsqueeze(1).broadcast_to([128, HALF_B, NP]), ALU.add).then_inc(s_hT, 1)

            def rope(half, w):
                n = 2 * half + w
                dve.wait_ge(s_qk_mm, n + 1)
                if n >= 2:
                    dve.wait_ge(s_rope, n - 1)
                b0 = 4 * (1 - half) + 2 * w
                for j, (eo, table) in enumerate(((0, cos8), (1, sin8), (1, cos8), (0, sin8))):
                    last = dve.scalar_tensor_tensor(out=per_image(rope_t[:, n % 2, j, :], T), in0=per_image(bank[:, b0 + eo, 0:HALF_T], T),
                                                    scalar=vec[:, (V_BQ, V_BK)[w] + eo:(V_BQ, V_BK)[w] + eo + 1],
                                                    in1=table, op0=ALU.add, op1=ALU.mult)
                last.then_inc(s_rope_mul, 1)

            def masked(g):
                n = GROUP[g]
                dve.wait_ge(s_score_mm, g // 2 + 1)
                dve.tensor_tensor_reduce(out=score[0:n, g, 0:n], in0=bank[0:n, (7, 0, 1)[g // 2], (g % 2) * 128:(g % 2) * 128 + n],
                                         in1=mask[0:n, 0:n], scale=1.0 / np.sqrt(D), scalar=-3e38, op0=ALU.add, op1=ALU.max,
                                         accum_out=top[0:n, g:g + 1]).then_inc(s_score, 1)

            def negated(g):
                n = GROUP[g]
                dve.wait_ge(s_score, g + 1)
                dve.tensor_scalar(neg_top[0:n, g:g + 1], top[0:n, g:g + 1], -1.0, None, ALU.mult).then_inc(s_neg_top, 1)

            def rows_in(g):
                n = GROUP[g]
                dve.wait_ge(s_row_mm, g // 2 + 1)
                dve.tensor_tensor(resid[0:n, g, :], bank[0:n, (2, 3, 7)[g // 2], (g % 2) * D:(g % 2 + 1) * D], bias_rows[0:n, :],
                                  ALU.add).then_inc(s_resid, 1)

            for w in range(2):
                rope(0, w)
            for w in range(2):
                rope(1, w)
            for g in range(2):
                masked(g)
            for g in range(2):
                negated(g)
            dve.wait_ge(s_cb_mm, 1)
            dve.wait_ge(s_bias, 32)
            dve.tensor_tensor(bias_rows[:], bank[0:GT, 4, 0:D], bf_rows[:], ALU.add).then_inc(s_cb, 1)
            dve.wait_ge(s_cb, 1)
            for g in range(2):
                rows_in(g)
            for g in range(2, NG):
                masked(g)
                if g >= 3:
                    negated(g - 1)
            negated(NG - 1)
            for g in range(2, NG):
                rows_in(g)

            def residual(g):
                n = GROUP[g]
                dve.wait_ge(s_prob, g + 1)
                link(dve.reciprocal(prob_inv[0:n, g:g + 1], prob_sum[0:n, g:g + 1]))
                dve.wait_ge(s_proj_mm, g + 1)
                dve.scalar_tensor_tensor(out=pre[0:n, g, :], in0=bank[0:n, WF_BANK[g % 2], 0:D], scalar=prob_inv[0:n, g:g + 1],
                                         in1=resid[0:n, g, :], op0=ALU.mult, op1=ALU.add).then_inc(s_pre, 1)
                dve.wait_ge(s_pre, g + 1)
                link(dve.bn_stats(stats[0:n, g, :], pre[0:n, g, :]))
                dve.bn_aggr(mv[0:n, g, :], stats[0:n, g, :]).then_inc(s_mv, 1)

            def normalise(g):
                n = GROUP[g]
                dve.wait_ge(s_std, g + 1)
                link(dve.reciprocal(rstd[0:n, g:g + 1], std[0:n, g:g + 1]))
                dve.tensor_scalar(h1[0:n, g, :], pre[0:n, g, :], mv[0:n, g, 0:1], rstd[0:n, g:g + 1],
                                  ALU.subtract, ALU.mult).then_inc(s_h1, 1)

            def route(b):
                g0, g1 = BATCHES[b]
                dve.wait_ge(s_logit_mm, b + 1)
                whole = g1 - 1 if g1 == NG else g1
                last = dve.tensor_copy(logit[:, g0:whole, :], bank[0:GT, (5, 1)[b], 0:(whole - g0) * E].rearrange("p (g e) -> p g e", e=E))
                if g1 == NG:
                    n = GROUP[whole]
                    last = dve.tensor_copy(logit[0:n, whole, :], bank[0:n, (5, 1)[b], (whole - g0) * E:(g1 - g0) * E])
                link(last)
                shape = [GT, g1 - g0, E, E]
                other, own = logit[:, g0:g1, :].unsqueeze(2).broadcast_to(shape), logit[:, g0:g1, :].unsqueeze(3).broadcast_to(shape)
                dve.tensor_tensor(above[:, g0:g1], other, own, ALU.is_gt)
                link(dve.tensor_tensor(equal[:, g0:g1], other, own, ALU.is_equal))
                link(dve.tensor_tensor(equal[:, g0:g1], equal[:, g0:g1], lower.unsqueeze(1).broadcast_to(shape), ALU.mult))
                link(dve.tensor_tensor(above[:, g0:g1], above[:, g0:g1], equal[:, g0:g1], ALU.add))
                link(dve.tensor_reduce(rank[:, g0:g1, :], above[:, g0:g1], AX_X, ALU.add))
                dve.tensor_scalar(picked_b[:, g0:g1, :], rank[:, g0:g1, :], 1.5, None, ALU.is_lt).then_inc(s_picked, 1)
                link(dve.tensor_scalar(picked[:, g0:g1, :], rank[:, g0:g1, :], 1.5, None, ALU.is_lt))

            def slots(b):
                g0, g1 = BATCHES[b]
                dve.wait_ge(s_pos_mm, b + 1)
                ahead = bank[0:GT, (7, 0)[b], 0:(g1 - g0) * E].rearrange("p (g e) -> p g e", e=E)
                link(dve.scalar_tensor_tensor(out=pos1[:, g0:g1, :], in0=ahead, scalar=1.0, in1=picked[:, g0:g1, :],
                                              op0=ALU.add, op1=ALU.mult))
                dve.tensor_scalar(slot_of[:, g0:g1, :], pos1[:, g0:g1, :], -1.0, None, ALU.add).then_inc(s_slot, 1)

            dve.wait_ge(s_setup, 4)
            for g in range(NG):
                residual(g)
                if g >= 1:
                    normalise(g - 1)
            normalise(NG - 1)
            route(0)
            slots(0)

            def select(e, par, groups):
                for g in groups:
                    last = dve.tensor_scalar(sel[:, par, g, :], iota, slot_of[:, g, bass.ds(e, 1)], None, ALU.is_equal)
                return last

            def slot_index(par, done):
                numbers = bank[0:SLOT_T, 7, 0:2 * ST].rearrange("p (t c) -> p t c", c=2)
                with whole_numbers():
                    return dve.tensor_reduce(tok_idx[:, par, :, 0], numbers, AX_X, ALU.add).then_inc(done, 1)

            def rows_to_sbuf(e, par):
                dve.wait_ge(s_xT_mm, e + 1)
                dve.tensor_copy(xT[:, par].rearrange("p k t -> p (k t)"), bank[:, 5, 0:DT * SLOTS]).then_inc(s_x, 1)

            route(1)
            dve.wait_ge(s_slot, 1)
            select(0, 0, range(*BATCHES[0]))
            slots(1)
            dve.wait_ge(s_slot, 2)
            select(0, 0, range(*BATCHES[1])).then_inc(s_sel, 1)
            select(1, 1, range(NG)).then_inc(s_sel, 1)
            dve.wait_ge(s_idx_mm, 1)
            slot_index(0, s_idx)
            dve.wait_ge(s_idx_mm, 2)
            slot_index(1, s_idx)
            tail_cols = (NG - BATCHES[1][0]) * E
            link(dve.tensor_copy(count_f[:], bank[0:1, 0, tail_cols:tail_cols + E]))
            dve.tensor_copy(count[:], count_f[:])
            with whole_numbers():
                dve.reduce_max(most[0:1, 0:1], count_f[:], AX_X).then_inc(s_count, 1)
            rows_to_sbuf(0, 0)

            def expert(i, par, gather_next, next_rows):
                e = 2 * i + par
                for m in range(MT):
                    dve.wait_ge(s_silu, MT * e + m + 1)
                    dve.tensor_tensor(hid[:, m, :], gated[:, m % 2, :], bank[:, m % 4, SLOTS:2 * SLOTS], ALU.mult).then_inc(s_hid, 1)
                    if gather_next and m == 3:
                        select(e + 2, par, range(NG)).then_inc(s_sel, 1)
                if next_rows:
                    rows_to_sbuf(e + 1, 1 - par)
                if gather_next:
                    dve.wait_ge(s_idx_mm, e + 3)
                    slot_index(par, s_idx)

            with dve.Fori(0, LAST_PAIR) as i:
                for par in range(2):
                    expert(i, par, True, True)

            dve.tensor_scalar(first[:], rank[:], 0.5, None, ALU.is_lt)
            link(dve.tensor_tensor(row_of[:], slot_of[:], row0.unsqueeze(1).broadcast_to([GT, NG, E]), ALU.add))
            dve.tensor_scalar(row_early[:], slot_of[:], float(SLOTS), None, ALU.is_lt)
            link(dve.tensor_tensor(second[:], picked[:], first[:], ALU.subtract))
            link(dve.tensor_tensor(row_early[:], row_early[:], row_of[:], ALU.mult))
            for c in range(1, PASSES):
                link(dve.tensor_scalar(pos1[:], slot_of[:], float(c * SLOTS), float(PASS_ROWS - SLOTS), ALU.is_ge, ALU.mult))
                link(dve.tensor_tensor(row_of[:], row_of[:], pos1[:], ALU.add))
            for k, which in enumerate((first, second)):
                dve.tensor_tensor(pick_t[:, k], row_of[:], which[:], ALU.mult)
                dve.tensor_tensor(pick_t[:, 4 + k], row_early[:], which[:], ALU.mult)
                link(dve.tensor_tensor(pick_t[:, 2 + k], logit[:], which[:], ALU.mult))
            for k in range(2):
                with whole_numbers():
                    dve.tensor_reduce(row_idx[:, k, :], pick_t[:, k], AX_X, ALU.add)
                    dve.tensor_reduce(early_idx[:, k, :], pick_t[:, 4 + k, :, 0:E - 1], AX_X, ALU.add)
                last = dve.tensor_reduce((l1, l2)[k][:], pick_t[:, 2 + k], AX_X, ALU.add)
            link(last)
            dve.tensor_tensor(gap[:], l1[:], l2[:], ALU.subtract).then_inc(s_gap, 1)
            dve.wait_ge(s_gap, 1)
            dve.memset(last_w[:], 0.0).then_inc(s_rows, 1)

            expert(LAST_PAIR, 0, False, True)
            expert(LAST_PAIR, 1, False, False)

            dve.wait_ge(s_tanh, 1)
            dve.wait_ge(s_rows, 1)
            dve.tensor_scalar(route_w[:, 0, :], tanh_gap[:], 0.5, 0.5, ALU.mult, ALU.add)
            link(dve.tensor_scalar(route_w[:, 1, :], tanh_gap[:], -0.5, 0.5, ALU.mult, ALU.add))
            dve.tensor_tensor(last_w[:, 1, :], route_w[:, 0, :], first[:, :, E - 1], ALU.mult)
            link(dve.tensor_tensor(last_w[:, 2, :], route_w[:, 1, :], second[:, :, E - 1], ALU.mult))
            link(dve.tensor_tensor(last_w[:, 0, :], last_w[:, 1, :], last_w[:, 2, :], ALU.add))

            def weighted(g, done, linked_by):
                n = GROUP[g]
                link(dve.scalar_tensor_tensor(out=mix2[0:n, g, :], in0=y_tok[0:n, 0, g, :], scalar=route_w[0:n, 0, g:g + 1],
                                              in1=h1[0:n, g, :], op0=ALU.mult, op1=ALU.add), linked_by)
                last = dve.scalar_tensor_tensor(out=mix[0:n, g, :], in0=y_tok[0:n, 1, g, :], scalar=route_w[0:n, 1, g:g + 1],
                                                in1=mix2[0:n, g, :], op0=ALU.mult, op1=ALU.add)
                last.then_inc(done, 1)

            for g in range(NG):
                dve.wait_ge(s_y_tok[g], 32)
                weighted(g, s_mix, s_link)
            dve.wait_ge(s_mix, NG)

            with further_passes(dve):
                all_stored(dve)
                with dve.Fori(0, E) as e:
                    for c in range(MORE):
                        n = e * MORE + c
                        dve.tensor_scalar(pos1[:, :, 0], slot_of[:, :, bass.ds(e, 1)].rearrange("p g o -> p (g o)"),
                                          -float(SLOTS * (c + 1)), None, ALU.add).then_inc(o_slot, 1)
                        dve.wait_ge(o_slot, n + 1)
                        dve.tensor_tensor(sel[:, 0], iota.unsqueeze(1).broadcast_to([GT, NG, SLOTS]),
                                          pos1[:, :, 0:1].broadcast_to([GT, NG, SLOTS]), ALU.is_equal).then_inc(o_sel, 1)
                        dve.wait_ge(o_idx_mm, n + 1)
                        slot_index(0, o_idx)
                        dve.wait_ge(o_xT_mm, n + 1)
                        dve.tensor_copy(xT[:, 0].rearrange("p k t -> p (k t)"), bank[:, 5, 0:DT * SLOTS]).then_inc(o_x, 1)
                        for m in range(MT):
                            dve.wait_ge(o_silu, MT * n + m + 1)
                            dve.tensor_tensor(hid[:, m, :], gated[:, m % 2, :], bank[:, m % 4, SLOTS:2 * SLOTS],
                                              ALU.mult).then_inc(o_hid, 1)
                        dve.wait_ge(o_yr, n + 1)
                dve.wait_ge(o_y_tok, 32 * NG)
                for g in range(NG):
                    weighted(g, o_slot, o_link)
                dve.wait_ge(o_slot, E * MORE + NG)
                dve.memset(last_w[:, 0, :], 0.0).then_inc(o_slot, 1)
                dve.wait_ge(o_slot, E * MORE + NG + 1)

            for g in range(NG):
                n = GROUP[g]
                dve.wait_ge(s_last_mm, g + 1)
                dve.scalar_tensor_tensor(out=mix2[0:n, g, :], in0=bank[0:n, g % 4, 0:D], scalar=last_w[0:n, 0, g:g + 1],
                                         in1=mix[0:n, g, :], op0=ALU.mult, op1=ALU.add).then_inc(s_mix2, 1)
                dve.wait_ge(s_mix2, g + 1)
                link(dve.bn_stats(stats[0:n, g, :], mix2[0:n, g, :]))
                dve.bn_aggr(mv[0:n, g, :], stats[0:n, g, :]).then_inc(s_mv2, 1)
                for d in ([g - 1] if g else []) + ([g] if g == NG - 1 else []):
                    n = GROUP[d]
                    dve.wait_ge(s_std2, d + 1)
                    link(dve.reciprocal(rstd[0:n, d:d + 1], std[0:n, d:d + 1]))
                    dve.tensor_scalar(out_sb[0:n, d, :], mix2[0:n, d, :], mv[0:n, d, 0:1], rstd[0:n, d:d + 1],
                                      ALU.subtract, ALU.mult).then_inc(s_out, 1)


def kernel(x, L0_tok_W, L0_tok_b, L0_tok_class_token, L0_tok_pos_embedding, L0_attn_Wq, L0_attn_bq, L0_attn_Wk,
           L0_attn_bk, L0_attn_Wv, L0_attn_bv, L0_attn_Wf, L0_attn_bf, L0_ffn_gate, L0_ffn_experts_w1,
           L0_ffn_experts_w2, L0_ffn_experts_w3):
    import concourse.bacc as bacc
    from concourse.bass_utils import run_bass_kernel_spmd

    def tiles(a):
        return a.reshape(-1, 128, a.shape[-1]).transpose(1, 0, 2)

    def columns(a):
        return np.asarray(a).reshape(DT, 128).T

    x = np.asarray(x)
    pt = x.reshape(B, CH, GRID, PATCH, GRID, PATCH).transpose(1, 3, 5, 0, 2, 4).reshape(KP // 2, 2, 128, 2, HALF_P)
    pt = pt.transpose(3, 0, 2, 1, 4)
    tw = np.asarray(L0_tok_W).T.reshape(KP // 2, 2, 128, D).transpose(0, 2, 1, 3)
    order = np.concatenate([np.arange(0, D, 2), np.arange(1, D, 2)])
    aw = np.stack([tiles(np.asarray(L0_attn_Wq)[order].T), tiles(np.asarray(L0_attn_Wk)[order].T),
                   tiles(np.asarray(L0_attn_Wv).T), tiles(np.asarray(L0_attn_Wf).T)], axis=1)
    pos = np.asarray(L0_tok_pos_embedding).reshape(T, DT, 128).transpose(2, 1, 0).reshape(128, DT * T)
    vecs = np.concatenate([columns(np.asarray(L0_attn_bq)[order]), columns(np.asarray(L0_attn_bk)[order]),
                           columns(L0_tok_b), columns(np.asarray(L0_tok_class_token).reshape(D)), columns(L0_attn_bv), pos], axis=1)

    def up(w):
        return np.asarray(w).reshape(E, DT, 128, INNER).transpose(0, 2, 1, 3).reshape(E, 128, DT * INNER)

    arrays = {
        "patches": pt, "tok_w": tw, "vecs": vecs, "attn_w": aw, "bf": np.asarray(L0_attn_bf),
        "gate": tiles(np.asarray(L0_ffn_gate)), "w1": up(L0_ffn_experts_w1), "w3": up(L0_ffn_experts_w3),
        "w2": np.asarray(L0_ffn_experts_w2).reshape(E, MT, 128, D).transpose(0, 2, 1, 3), "consts": shape_constants(),
    }
    arrays = {k: np.ascontiguousarray(v) for k, v in arrays.items()}
    nc = bacc.Bacc("TRN2", target_bir_lowering=False, num_devices=1)
    args = [nc.dram_tensor(k, v.shape, mybir.dt.from_np(v.dtype), kind="ExternalInput").ap() for k, v in arrays.items()]
    out = nc.dram_tensor("out", (B, T, D), F32, kind="ExternalOutput").ap()
    vit_layer(nc, *args, out)
    r = run_bass_kernel_spmd(nc, [arrays], core_ids=[0])
    return r.results[0]["out"]
```

```python
from contextlib import ExitStack

import numpy as np

import concourse.bass as bass
from concourse import mybir

ALU = mybir.AluOpType
ACT = mybir.ActivationFunctionType
AX_X = mybir.AxisListType.X
F32 = mybir.dt.float32
BF16 = mybir.dt.bfloat16
U32 = mybir.dt.uint32
I32 = mybir.dt.int32

B, CH, IMG, PATCH = 16, 3, 96, 16
GRID = IMG // PATCH
NP = GRID * GRID
T = NP + 1
TOK = B * T
D = 256
DT = D // 128
KP = CH * PATCH * PATCH // 128
HALF_B = B // 2
HALF_P, HALF_T = HALF_B * NP, HALF_B * T
GB = 128 // T
GT = GB * T
NG = -(-B // GB)
GROUP = [min(GT, TOK - g * GT) for g in range(NG)]
E, INNER = 8, 1024
MT = INNER // 128
SLOTS = 208
ST = 2
SLOT_T = SLOTS // ST
PASSES = -(-TOK // SLOTS)
PASS_ROWS = E * SLOTS
LAST_ROW = 1 + (E - 1) * SLOTS
FIRST_ROWS = LAST_ROW - SLOTS
SPLIT = NG // 2
BATCHES = ((0, SPLIT), (SPLIT, NG))
EPS = 1e-5
REST = NG + 1 - BATCHES[1][0]
NEG = -1e30
WIDTHS = (SLOTS - 72, SLOTS - 48, SLOTS - 24, SLOTS)
BY_VECTOR = (NG - 2, NG - 1)
WARM = 9
GROUP_WARM, ROUTE_WARM, SELECT_WARM = 1, 4, 3

C_ID = 0
C_MASK = C_ID + 128
C_TRI = C_MASK + GT
C_COS = C_TRI + GT
C_SIN = C_COS + T
C_IOTA = C_SIN + T
C_ROW0 = C_IOTA + SLOTS
C_LT = C_ROW0 + E
C_TID = C_LT + E * E
C_W = C_TID + 2 * NG

V_BQ, V_BK, V_BT, V_CLS, V_BV, V_POS = 0, DT, 2 * DT, 3 * DT, 4 * DT, 5 * DT
V_W = V_POS + DT * T


def shape_constants():
    c = np.zeros((128, C_W), np.float32)
    c[:, C_ID:C_ID + 128] = np.eye(128)
    p, q = np.arange(GT)[:, None], np.arange(GT)[None, :]
    c[:GT, C_MASK:C_MASK + GT] = np.where((p // T == q // T) & (q <= p), 0.0, NEG)
    c[:GT, C_TRI:C_TRI + GT] = p < q
    freqs = (np.float32(1.0) / np.float32(10000.0) ** (np.arange(0, D, 2, dtype=np.float32) / np.float32(D)))
    ang = freqs.astype(np.float32)[:, None] * np.arange(T, dtype=np.float32)[None, :]
    c[:, C_COS:C_COS + T] = np.cos(ang)
    c[:, C_SIN:C_SIN + T] = np.sin(ang)
    c[:, C_IOTA:C_IOTA + SLOTS] = 1 + np.arange(SLOTS)
    c[:, C_ROW0:C_ROW0 + E] = np.arange(E) * SLOTS
    e, f = np.arange(E)[:, None], np.arange(E)[None, :]
    c[:, C_LT:C_LT + E * E] = (f < e).reshape(-1)
    for g in range(NG):
        token = g * GT + np.arange(128)
        c[:, C_TID + 2 * g] = token // 4 * 4
        c[:, C_TID + 2 * g + 1] = token % 4
    return c


def vit_layer(nc, patches, tok_w, vecs, attn_w, bf, gate, w1, w3, w2, consts, out):
    h1_dram = nc.dram_tensor("h1_rows", (TOK, D), F32, kind="Internal").ap()
    y_dram = nc.dram_tensor("expert_rows", (1 + PASSES * PASS_ROWS, D), F32, kind="Internal").ap()
    out_rows = out.rearrange("b j d -> (b j) d")

    with ExitStack() as ctx:
        def sb(name, shape, dt=F32):
            return ctx.enter_context(nc.sbuf_tensor(name, shape, dt))

        def sem(name):
            return ctx.enter_context(nc.semaphore(name))

        bank = ctx.enter_context(nc.psum_tensor("bank", [128, 8, 512], F32))

        cst = sb("cst", [128, C_W])
        vec = sb("vec", [128, V_W])
        bf_rows = sb("bf_rows", [GT, D])
        tok_w_sb = sb("tok_w_sb", [128, KP, D])
        patch_sb = sb("patch_sb", [128, 2, KP, HALF_P])
        attn_w_sb = sb("attn_w_sb", [128, 4, DT, D])
        gate_sb = sb("gate_sb", [128, DT, E])
        ident = cst[:, C_ID:C_ID + 128]
        mask = cst[0:GT, C_MASK:C_MASK + GT]
        iota = cst[0:GT, C_IOTA:C_IOTA + SLOTS]
        row0 = cst[0:GT, C_ROW0:C_ROW0 + E]
        lower = sb("lower", [GT, E, E], BF16)
        tri_b = sb("tri_b", [GT, GT], BF16)
        ones_b = sb("ones_b", [GT, GT], BF16)
        tid_b = sb("tid_b", [GT, NG, 2], BF16)
        ident_b = sb("ident_b", [GT, GT], BF16)
        warm_b = sb("warm_b", [128, 512], BF16)
        eps_col = sb("eps_col", [GT, 1])
        unread = sb("unread", [1, 3])
        zero_row = sb("zero_row", [1, D])

        posb = sb("posb", [128, DT, T])
        bv_b = sb("bv_b", [128, DT, GT])
        bias_rows = sb("bias_rows", [GT, D])
        hT = sb("hT", [128, DT, TOK])
        rope_t = sb("rope_t", [128, 2, 4, HALF_T])
        qk = sb("qk", [128, 2, 2, TOK])
        v_sb = sb("v_sb", [GT, NG, D])
        resid = sb("resid", [GT, NG, D])
        score = sb("score", [GT, NG, GT])
        prob = sb("prob", [GT, NG, GT])
        probT = sb("probT", [GT, 2, GT])
        vf_w = sb("vf_w", [128, DT, D])
        top = sb("top", [GT, NG])
        neg_top = sb("neg_top", [GT, NG])
        prob_sum = sb("prob_sum", [GT, NG])
        prob_inv = sb("prob_inv", [GT, NG])
        pre = sb("pre", [GT, NG, D])
        stats = sb("stats", [GT, NG, 6])
        mv = sb("mv", [GT, NG, 2])
        std = sb("std", [GT, NG])
        rstd = sb("rstd", [GT, NG])
        shift = sb("shift", [GT, NG])
        h1 = sb("h1", [GT, NG, D])
        h1T = sb("h1T", [128, NG, DT, GT])

        logit = sb("logit", [GT, NG, E])
        above = sb("above", [GT, NG, E, E], BF16)
        equal = sb("equal", [GT, NG, E, E], BF16)
        rank = sb("rank", [GT, NG, E])
        picked = sb("picked", [GT, NG, E])
        picked_b = sb("picked_b", [GT, NG, E], BF16)
        first = sb("first", [GT, NG, E])
        second = sb("second", [GT, NG, E])
        pos1 = sb("pos1", [GT, NG, E])
        place = sb("place", [GT, NG, E])
        row_of = sb("row_of", [GT, NG, E])
        row_early = sb("row_early", [GT, NG, E])
        pick_t = sb("pick_t", [GT, 6, NG, E])
        low = sb("low", [GT, NG, E])
        high = sb("high", [GT, NG, E])
        early = sb("early", [GT, 2, NG, E])
        row_idx = sb("row_idx", [GT, 2, NG], U32)
        early_idx = sb("early_idx", [GT, 2, NG], U32)
        count_f = sb("count_f", [1, E])
        count = sb("count", [1, E], I32)
        most = sb("most", [1, 1], I32)
        l1 = sb("l1", [GT, NG])
        l2 = sb("l2", [GT, NG])
        gap = sb("gap", [GT, NG])
        tanh_gap = sb("tanh_gap", [GT, NG])
        choice_w = sb("choice_w", [GT, 2, NG])
        weight_t = sb("weight_t", [GT, 2, NG, E])
        expert_w = sb("expert_w", [GT, NG, E])
        weighted_t = sb("weighted_t", [GT, 4, NG, E])
        pair_w = sb("pair_w", [GT, 4, NG])
        last_w = sb("last_w", [GT, NG])
        sel0 = rope_t[0:GT].rearrange("p a b c -> p (a b c)")[:, 0:NG * SLOTS].rearrange("p (g s) -> p g s", g=NG)
        sel = sb("sel", [GT, 2, NG, SLOTS], BF16)
        selT = sb("selT", [SLOT_T, ST, NG, GT])
        tok_idx = sb("tok_idx", [SLOT_T, 2, ST, 1], U32)

        w13_sb = sb("w13_sb", [128, 2, 2, DT * INNER])
        w2_sb = sb("w2_sb", [128, 2, MT, D])
        xg = sb("xg", [SLOT_T, 2, ST, D])
        xT = sb("xT", [128, 2, DT, SLOTS])
        gated = sb("gated", [128, 2, SLOTS])
        hid = sb("hid", [128, MT, SLOTS])
        yT = sb("yT", [128, DT, SLOTS])
        y_sb = sb("y_sb", [SLOT_T, 2, ST, D])
        y_tok = sb("y_tok", [GT, 2, NG, D])
        mix = sb("mix", [GT, NG, D])
        mix2 = v_sb
        out_sb = pre

        s_front = [sem(f"s_front{k}") for k in range(KP // 2)]
        s_patch1 = sem("s_patch1")
        s_small = sem("s_small")
        s_attn_w = sem("s_attn_w")
        s_bias = sem("s_bias")
        s_w13 = [sem(f"s_w13_{p}") for p in range(2)]
        s_w2 = [sem(f"s_w2_{p}") for p in range(2)]
        s_zero_row = sem("s_zero_row")
        s_warm = sem("s_warm")
        s_setup = sem("s_setup")
        s_link = sem("s_link")
        s_const = sem("s_const")
        s_patch_mm = sem("s_patch_mm")
        s_hT = sem("s_hT")
        s_qk_mm = sem("s_qk_mm")
        s_rope_mul = sem("s_rope_mul")
        s_rope = sem("s_rope")
        s_v_mm = sem("s_v_mm")
        s_v = sem("s_v")
        s_cb_mm = sem("s_cb_mm")
        s_cb = sem("s_cb")
        s_score_mm = sem("s_score_mm")
        s_score = sem("s_score")
        s_neg_top = sem("s_neg_top")
        s_prob = sem("s_prob")
        s_row_mm = sem("s_row_mm")
        s_resid = sem("s_resid")
        s_probT_mm = sem("s_probT_mm")
        s_probT = sem("s_probT")
        s_vf_w_mm = sem("s_vf_w_mm")
        s_vf_w = sem("s_vf_w")
        s_attn_mm = sem("s_attn_mm")
        s_prob_inv = sem("s_prob_inv")
        s_pre = sem("s_pre")
        s_mv = sem("s_mv")
        s_std = sem("s_std")
        s_rstd = sem("s_rstd")
        s_shift = sem("s_shift")
        s_h1 = sem("s_h1")
        s_h1_late = sem("s_h1_late")
        s_h1_dram = sem("s_h1_dram")
        s_h1T_mm = sem("s_h1T_mm")
        s_h1T = sem("s_h1T")
        s_logit_mm = sem("s_logit_mm")
        s_picked = sem("s_picked")
        s_pos_mm = sem("s_pos_mm")
        s_place = sem("s_place")
        s_count = sem("s_count")
        s_rows = sem("s_rows")
        s_gap = sem("s_gap")
        s_tanh = sem("s_tanh")
        s_sel0 = sem("s_sel0")
        s_x0_mm = sem("s_x0_mm")
        s_x0 = sem("s_x0")
        s_sel = sem("s_sel")
        s_idx_mm = sem("s_idx_mm")
        s_idx = sem("s_idx")
        s_gathers = sem("s_gathers")
        s_xg = [sem(f"s_xg{p}") for p in range(2)]
        s_xT_mm = sem("s_xT_mm")
        s_x = sem("s_x")
        s_gu_mm = sem("s_gu_mm")
        s_silu = sem("s_silu")
        s_hid = sem("s_hid")
        s_y_mm = sem("s_y_mm")
        s_y = sem("s_y")
        s_yT_mm = sem("s_yT_mm")
        s_yr = sem("s_yr")
        s_y_dram = [sem(f"s_y_dram{p}") for p in range(2)]
        s_selT_mm = sem("s_selT_mm")
        s_selT = sem("s_selT")
        s_y_tok0 = [sem(f"s_y_tok0_{g}") for g in range(NG)]
        s_y_tok = [sem(f"s_y_tok{g}") for g in range(NG)]
        s_partly = sem("s_partly")
        s_mix = sem("s_mix")
        s_last_mm = sem("s_last_mm")
        s_mix2 = sem("s_mix2")
        s_mv2 = sem("s_mv2")
        s_std2 = sem("s_std2")
        s_rstd2 = sem("s_rstd2")
        s_shift2 = sem("s_shift2")
        s_out = sem("s_out")
        s_out_late = sem("s_out_late")
        s_out_dram = sem("s_out_dram")
        o_w = sem("o_w")
        o_slot = sem("o_slot")
        o_sel = sem("o_sel")
        o_idx_mm = sem("o_idx_mm")
        o_idx = sem("o_idx")
        o_xg = sem("o_xg")
        o_xT_mm = sem("o_xT_mm")
        o_x = sem("o_x")
        o_gu_mm = sem("o_gu_mm")
        o_silu = sem("o_silu")
        o_hid = sem("o_hid")
        o_y_mm = sem("o_y_mm")
        o_y = sem("o_y")
        o_yT_mm = sem("o_yT_mm")
        o_yr = sem("o_yr")
        o_y_dram = sem("o_y_dram")
        o_y_tok = sem("o_y_tok")
        o_partly = sem("o_partly")
        o_mix = sem("o_mix")

        cos8 = cst[:, C_COS:C_COS + T].unsqueeze(1).broadcast_to([128, HALF_B, T])
        sin8 = cst[:, C_SIN:C_SIN + T].unsqueeze(1).broadcast_to([128, HALF_B, T])

        def per_image(ap, n):
            return ap.rearrange("p (b j) -> p b j", j=n)

        def further_passes(eng):
            return eng.If(eng.value_load(most[0:1, 0:1], min_val=0, max_val=TOK) > SLOTS)

        def whole_numbers():
            return nc.allow_low_precision(reason="sums of whole numbers below 2**24, kept as integers")

        def all_stored(eng):
            for par in range(2):
                eng.wait_ge(s_y_dram[par], 16 * (E // 2))

        def finished(eng, g, by_scalar, by_vector):
            if g in BY_VECTOR:
                eng.wait_ge(by_vector, BY_VECTOR.index(g) + 1)
            else:
                eng.wait_ge(by_scalar, g + 1)

        MORE = PASSES - 1
        LAST_PAIR = E // 2 - 1
        VALUE_BANK = (5, 6, 6)
        SCORE_BANK = (7, 0, 1)
        ROW_BANK = (2, 3, 7)
        PROB_BANK = (0, 1)
        ATTN_BANK = (4, 5)
        H1T_BANK = (3, 2)
        LOGIT_BANK = (6, 7)
        AHEAD_BANK = (1, 0)
        LAST_Y_BANK = (4, 0)
        LAST_ROW_BANK = (6, 5)

        block = ctx.enter_context(nc.Block())

        @block.sync
        def _(sp):
            for k in range(KP // 2):
                sp.dma_start(tok_w_sb[:, 2 * k:2 * k + 2, :], tok_w[k]).then_inc(s_front[k], 16)
                sp.dma_start(patch_sb[:, 0, 2 * k:2 * k + 2, :], patches[0, k]).then_inc(s_front[k], 16)
            sp.dma_start(vec[:], vecs).then_inc(s_small, 16)
            sp.dma_start(cst[:], consts).then_inc(s_small, 16)
            for k in range(KP // 2):
                sp.dma_start(patch_sb[:, 1, 2 * k:2 * k + 2, :], patches[1, k]).then_inc(s_patch1, 16)
            sp.dma_start(attn_w_sb[:], attn_w).then_inc(s_attn_w, 16)
            sp.dma_start(gate_sb[:], gate).then_inc(s_bias, 16)
            sp.dma_start(bf_rows[:], bf.partition_broadcast(GT)).then_inc(s_bias, 16)

            def load_w13(e, par):
                sp.dma_start(w13_sb[:, par, 0, :], w1[bass.ds(e, 1)].rearrange("o p c -> (o p) c")).then_inc(s_w13[par], 16)
                sp.dma_start(w13_sb[:, par, 1, :], w3[bass.ds(e, 1)].rearrange("o p c -> (o p) c")).then_inc(s_w13[par], 16)

            def load_w2(e, par):
                sp.dma_start(w2_sb[:, par], w2[bass.ds(e, 1)].rearrange("o p m d -> (o p) m d")).then_inc(s_w2[par], 16)

            for par in range(2):
                load_w13(par, par)
                load_w2(par, par)
            sp.wait_ge(s_setup, 4)
            sp.dma_start(y_dram[0:1, :], zero_row[:]).then_inc(s_zero_row, 16)
            for g in range(NG):
                finished(sp, g, s_h1, s_h1_late)
                sp.dma_start(h1_dram[g * GT:g * GT + GROUP[g], :], h1[0:GROUP[g], g, :]).then_inc(s_h1_dram, 16)

            def expert(i, par, load):
                e = 2 * i + par
                row = sp.snap(e * SLOTS + 1)
                if load:
                    sp.wait_ge(s_gu_mm, MT * e + MT)
                    load_w13(e + 2, par)
                    sp.wait_ge(s_y_mm, e + 1)
                    load_w2(e + 2, par)
                last = not load and par == 1
                sp.wait_ge(s_yr, E + 1 if last else e + 1)
                sp.dma_start(y_dram[bass.ds(row, SLOTS), :].rearrange("(t p) d -> p t d", p=SLOT_T),
                             y_sb[:, par]).then_inc(s_y_dram[par], 16)

            with sp.Fori(0, LAST_PAIR) as i:
                for par in range(2):
                    expert(i, par, True)
            for par in range(2):
                expert(LAST_PAIR, par, False)

            sp.wait_ge(s_count, 1)
            with further_passes(sp):
                with sp.Fori(0, E) as e:
                    for c in range(MORE):
                        n = e * MORE + c
                        all_stored(sp)
                        sp.dma_start(w13_sb[:, 0, 0, :], w1[bass.ds(e, 1)].rearrange("o p c -> (o p) c")).then_inc(o_w, 16)
                        sp.dma_start(w13_sb[:, 0, 1, :], w3[bass.ds(e, 1)].rearrange("o p c -> (o p) c")).then_inc(o_w, 16)
                        sp.dma_start(w2_sb[:, 0], w2[bass.ds(e, 1)].rearrange("o p m d -> (o p) m d")).then_inc(o_w, 16)
                        row = sp.snap(e * SLOTS + (1 + (c + 1) * PASS_ROWS))
                        sp.wait_ge(o_yr, n + 1)
                        sp.dma_start(y_dram[bass.ds(row, SLOTS), :].rearrange("(t p) d -> p t d", p=SLOT_T),
                                     y_sb[:, 0]).then_inc(o_y_dram, 16)
                sp.wait_ge(o_y_dram, 16 * E * MORE)
            for g in range(NG):
                finished(sp, g, s_out, s_out_late)
                sp.dma_start(out_rows[g * GT:g * GT + GROUP[g], :], out_sb[0:GROUP[g], g, :]).then_inc(s_out_dram, 16)
            sp.wait_ge(s_out_dram, 16 * NG)
            sp.wait_ge(s_h1_dram, 16 * NG)
            sp.wait_ge(s_zero_row, 16)
            all_stored(sp)

        @block.gpsimd
        def _(pool):
            pool.memset(ones_b[:], 1.0).then_inc(s_setup, 1)
            pool.memset(logit[:], 0.0).then_inc(s_setup, 1)
            pool.memset(y_sb[:], 0.0).then_inc(s_setup, 1)
            pool.memset(zero_row[:], 0.0).then_inc(s_setup, 1)
            for half in range(2):
                for w in range(2):
                    n = 2 * half + w
                    cols = slice(half * HALF_T, (half + 1) * HALF_T)
                    pool.wait_ge(s_rope_mul, n + 1)
                    pool.tensor_tensor(qk[:, w, 0, cols], rope_t[:, n % 2, 0, :], rope_t[:, n % 2, 1, :], ALU.subtract)
                    pool.tensor_tensor(qk[:, w, 1, cols], rope_t[:, n % 2, 2, :], rope_t[:, n % 2, 3, :],
                                       ALU.add).then_inc(s_rope, 1)

            def shifts(groups, std_inverted, done):
                for g in groups:
                    n = GROUP[g]
                    pool.wait_ge(std_inverted, g + 1)
                    pool.tensor_scalar(shift[0:n, g:g + 1], mv[0:n, g, 0:1], rstd[0:n, g:g + 1], -1.0,
                                       ALU.mult, ALU.mult).then_inc(done, 1)

            shifts(range(BY_VECTOR[0]), s_rstd, s_shift)

            def gather(e, par):
                pool.wait_ge(s_idx, e)
                pool.sem_inc(s_gathers, 1)
                for t in range(ST):
                    pool.indirect_dma_start(xg[:, par, t, :], None, h1_dram[:, :],
                                            bass.IndirectOffsetOnAxis(tok_idx[:, par, t, :], 0)).then_inc(s_xg[par], 16)

            pool.wait_ge(s_h1_dram, 16 * NG)
            gather(1, 1)
            with pool.Fori(0, LAST_PAIR) as i:
                for par in range(2):
                    e = 2 * i + par
                    gather(e + 2, par)

            def token_rows(k, idx, rows, done):
                for g in range(NG):
                    pool.indirect_dma_start(y_tok[0:GROUP[g], k, g, :], None, y_dram[0:rows, :],
                                            bass.IndirectOffsetOnAxis(idx[0:GROUP[g], k, g:g + 1], 0)).then_inc(done(g), 16)

            pool.wait_ge(s_rows, 1)
            pool.wait_ge(s_zero_row, 16)
            for par in range(2):
                pool.wait_ge(s_y_dram[par], 16 * (E // 2 - 1))
            token_rows(0, early_idx, FIRST_ROWS, lambda g: s_y_tok0[g])
            pool.wait_ge(s_y_dram[0], 16 * (E // 2))
            token_rows(1, early_idx, LAST_ROW, lambda g: s_y_tok[g])

            with further_passes(pool):
                all_stored(pool)
                with pool.Fori(0, E * MORE) as n:
                    pool.wait_ge(o_idx, n + 1)
                    pool.sem_inc(s_gathers, 1)
                    for t in range(ST):
                        pool.indirect_dma_start(xg[:, 0, t, :], None, h1_dram[:, :],
                                                bass.IndirectOffsetOnAxis(tok_idx[:, 0, t, :], 0)).then_inc(o_xg, 16)
                pool.wait_ge(o_y_dram, 16 * E * MORE)
                pool.wait_ge(s_mix, NG)
                for k in range(2):
                    token_rows(k, row_idx, 1 + PASSES * PASS_ROWS, lambda g: o_y_tok)

            shifts(range(BY_VECTOR[0]), s_rstd2, s_shift2)

        @block.tensor
        def _(pe):
            def keep_warm(n, banks):
                for k in range(n):
                    pe.matmul(bank[:, banks[k % len(banks)], :], warm_b[:, 0:128], warm_b[:], start=True, stop=True)

            pe.wait_ge(s_warm, 1)
            keep_warm(WARM, (7,))
            for half in range(2):
                for k in range(KP):
                    if half == 0 and k % 2 == 0:
                        pe.wait_ge(s_front[k // 2], 32)
                    if half == 1 and k == 0:
                        pe.wait_ge(s_patch1, 16 * (KP // 2))
                    for m in range(DT):
                        last = pe.matmul(bank[:, 2 * half + m, 0:HALF_P], tok_w_sb[:, k, m * 128:(m + 1) * 128],
                                         patch_sb[:, half, k, :], start=(k == 0), stop=(k == KP - 1))
                last.then_inc(s_patch_mm, 1)
            pe.wait_ge(s_attn_w, 16)
            for half in range(2):
                pe.wait_ge(s_hT, 1 + DT * (half + 1))
                for w in range(2):
                    for eo in range(2):
                        for k in range(DT):
                            last = pe.matmul(bank[:, 4 * (1 - half) + 2 * w + eo, 0:HALF_T],
                                             attn_w_sb[:, w, k, eo * 128:(eo + 1) * 128],
                                             hT[:, k, half * HALF_T:(half + 1) * HALF_T], start=(k == 0), stop=(k == DT - 1))
                    last.then_inc(s_qk_mm, 1)

            def cols(g):
                return slice(g * GT, g * GT + GROUP[g])

            def value_projection():
                for m in range(DT):
                    for k in range(DT):
                        last = pe.matmul(bank[:, 4, m * D:(m + 1) * D], attn_w_sb[:, 2, k, m * 128:(m + 1) * 128],
                                         attn_w_sb[:, 3, k, :], start=(k == 0), stop=(k == DT - 1))
                last.then_inc(s_vf_w_mm, 1)

            def values(g):
                n = GROUP[g]
                for k in range(DT):
                    last = pe.matmul(bank[0:n, VALUE_BANK[g // 2], (g % 2) * D:(g % 2 + 1) * D], hT[:, k, cols(g)], vf_w[:, k, :],
                                     start=(k == 0), stop=(k == DT - 1))
                if g % 2 == 1:
                    last.then_inc(s_v_mm, 1)

            def scores(j):
                for g in (2 * j, 2 * j + 1):
                    n = GROUP[g]
                    for eo in range(2):
                        last = pe.matmul(bank[0:n, SCORE_BANK[j], (g % 2) * 128:(g % 2) * 128 + n], qk[:, 0, eo, cols(g)],
                                         qk[:, 1, eo, cols(g)], start=(eo == 0), stop=(eo == 1))
                last.then_inc(s_score_mm, 1)

            def token_rows(j):
                for g in (2 * j, 2 * j + 1):
                    n = GROUP[g]
                    for k in range(DT):
                        last = pe.transpose(bank[0:n, ROW_BANK[j], (g % 2 * DT + k) * 128:(g % 2 * DT + k + 1) * 128],
                                            hT[:, k, cols(g)], ident)
                last.then_inc(s_row_mm, 1)

            pe.wait_ge(s_rope_mul, 2)
            value_projection()
            pe.wait_ge(s_const, 4)
            for k in range(DT):
                last = pe.matmul(bank[0:GT, 6, 0:D], bv_b[:, k, :], attn_w_sb[:, 3, k, :], start=(k == 0), stop=(k == DT - 1))
            last.then_inc(s_cb_mm, 1)
            pe.wait_ge(s_rope, 2)
            scores(0)
            pe.wait_ge(s_vf_w, 1)
            values(0)
            values(1)
            pe.wait_ge(s_rope_mul, 4)
            token_rows(0)
            pe.wait_ge(s_rope, 4)
            scores(1)
            scores(2)

            def probs_transposed(g):
                n = GROUP[g]
                pe.wait_ge(s_prob, g + 1)
                if g < 2:
                    pe.wait_ge(s_score, 4 + 2 * g)
                else:
                    pe.wait_ge(s_probT, g - 1)
                pe.transpose(bank[0:n, PROB_BANK[g % 2], 0:n], prob[0:n, g, 0:n], cst[0:n, C_ID:C_ID + n]).then_inc(s_probT_mm, 1)

            def attention(g):
                n = GROUP[g]
                pe.wait_ge(s_probT, g + 1)
                pe.wait_ge(s_v, g // 2 + 1)
                if g >= 2:
                    pe.wait_ge(s_pre, g - 1)
                pe.matmul(bank[0:n, ATTN_BANK[g % 2], 0:D], probT[0:n, g % 2, 0:n], v_sb[0:n, g, :],
                          start=True, stop=True).then_inc(s_attn_mm, 1)

            def h1_transposed(g):
                n = GROUP[g]
                finished(pe, g, s_h1, s_h1_late)
                if g < 2:
                    pe.wait_ge(s_resid, 4 - 2 * g)
                else:
                    pe.wait_ge(s_h1T, g - 1)
                for k in range(DT):
                    last = pe.transpose(bank[:, H1T_BANK[g % 2], k * 128:k * 128 + n], h1[0:n, g, k * 128:(k + 1) * 128],
                                        cst[0:n, C_ID:C_ID + n])
                last.then_inc(s_h1T_mm, 1)

            def logits(g):
                b = 0 if g < BATCHES[1][0] else 1
                n, c = GROUP[g], g - BATCHES[b][0]
                pe.wait_ge(s_h1T, g + 1)
                for k in range(DT):
                    last = pe.matmul(bank[0:n, LOGIT_BANK[b], c * E:(c + 1) * E], h1T[:, g, k, 0:n], gate_sb[:, k, :],
                                     start=(k == 0), stop=(k == DT - 1))
                if g + 1 == BATCHES[b][1]:
                    last.then_inc(s_logit_mm, 1)

            def ahead(b):
                g0, g1 = BATCHES[b]
                own = AHEAD_BANK[b]
                pe.wait_ge(s_picked, b + 1)
                if b == 0:
                    pe.wait_ge(s_probT, NG)
                end = g1 + 1 if g1 == NG else g1
                for g in range(g0, g1):
                    n, c = GROUP[g], g - g0
                    if g + 1 < end:
                        pe.matmul(bank[0:GT, own, (c + 1) * E:(end - g0) * E].rearrange("p (r e) -> p r e", e=E), ones_b[0:n, :],
                                  picked_b[0:n, g:g + 1, :].broadcast_to([n, end - g - 1, E]), start=(b == 0 and c == 0), stop=False)
                    last = pe.matmul(bank[0:GT, own, c * E:(c + 1) * E], tri_b[0:n, :], picked_b[0:n, g, :],
                                     start=False, stop=(g == g1 - 1))
                last.then_inc(s_pos_mm, 1)
                if b == 0:
                    for j in range(g1):
                        pe.matmul(bank[0:GT, AHEAD_BANK[1], 0:REST * E].rearrange("p (r e) -> p r e", e=E), ones_b[:],
                                  picked_b[:, j:j + 1, :].broadcast_to([GT, REST, E]), start=(j == 0), stop=False)

            def first_rows(groups):
                for g in groups:
                    n = GROUP[g]
                    pe.wait_ge(s_sel0, g + 1)
                    for m in range(DT):
                        last = pe.matmul(bank[:, 5 + m, 0:SLOTS], h1[0:n, g, m * 128:(m + 1) * 128], sel0[0:n, g, :],
                                         start=(g == 0), stop=(g == NG - 1))
                return last

            def slot_tokens(par):
                for t in range(ST):
                    for g in range(NG):
                        n = GROUP[g]
                        last = pe.matmul(bank[0:SLOT_T, 7, 2 * t:2 * t + 2], sel[0:n, par, g, t * SLOT_T:(t + 1) * SLOT_T],
                                         tid_b[0:n, g, :], start=(g == 0), stop=(g == NG - 1))
                return last

            def rows_transposed(par):
                for k in range(DT):
                    for t in range(ST):
                        last = pe.transpose(bank[:, 5, (k * ST + t) * SLOT_T:(k * ST + t + 1) * SLOT_T],
                                            xg[:, par, t, k * 128:(k + 1) * 128], cst[0:SLOT_T, C_ID:C_ID + SLOT_T])
                return last

            def y_rows():
                for t in range(ST):
                    for m in range(DT):
                        last = pe.transpose(bank[0:SLOT_T, 6, (t * DT + m) * 128:(t * DT + m + 1) * 128],
                                            yT[:, m, t * SLOT_T:(t + 1) * SLOT_T], ident)
                return last

            def gate_up(par, m, x, width):
                for which in range(2):
                    for k in range(DT):
                        c0 = k * INNER + m * 128
                        last = pe.matmul(bank[:, m % 4, which * SLOTS:which * SLOTS + width], w13_sb[:, par, which, c0:c0 + 128],
                                         x[:, k, 0:width], start=(k == 0), stop=(k == DT - 1))
                return last

            probs_transposed(0)
            pe.wait_ge(s_cb, 1)
            values(2)
            probs_transposed(1)
            values(3)
            attention(0)
            token_rows(1)
            pe.wait_ge(s_bias, 32)
            for g in range(NG + 3):
                if g + 2 < NG:
                    probs_transposed(g + 2)
                if g + 1 < NG:
                    attention(g + 1)
                if 2 <= g < 4:
                    pe.wait_ge(s_resid, 6)
                    keep_warm(GROUP_WARM, (7,))
                if g == 0:
                    pe.wait_ge(s_score, 2)
                    token_rows(2)
                if g == 1:
                    pe.wait_ge(s_v, 2)
                    values(4)
                    values(5)
                if 3 <= g:
                    h1_transposed(g - 3)
                if 4 <= g:
                    if g == 4:
                        pe.wait_ge(s_v, 3)
                        pe.wait_ge(s_resid, 6)
                    logits(g - 4)
                    if g < SPLIT + 4:
                        keep_warm(GROUP_WARM, (7,))
            logits(NG - 1)
            pe.wait_ge(s_pre, NG)
            keep_warm(ROUTE_WARM, (2, 3, 4))
            ahead(0)
            keep_warm(SELECT_WARM, (2, 3, 4))
            first_rows(range(SPLIT))
            pe.wait_ge(s_place, 1)
            keep_warm(1, (1,))
            ahead(1)
            keep_warm(SELECT_WARM, (2, 3, 4))
            first_rows(range(*BATCHES[1])).then_inc(s_x0_mm, 1)
            pe.wait_ge(s_count, 1)
            keep_warm(1, (0,))

            def rows_out(e):
                pe.wait_ge(s_y, e + 1)
                pe.wait_ge(s_yr, e)
                y_rows().then_inc(s_yT_mm, 1)

            def products(i, par, gather_next, next_rows, prev, width):
                e = 2 * i + par
                if prev:
                    pe.wait_ge(s_x, e)
                else:
                    pe.wait_ge(s_x0, DT)
                pe.wait_ge(s_w13[par], 32 * (i + 1))
                for m in range(MT):
                    if m >= 4 or prev:
                        pe.wait_ge(s_hid, MT * e + m - 3)
                    gate_up(par, m, xT[:, par], width).then_inc(s_gu_mm, 1)
                    if m == 1:
                        if prev:
                            rows_out(e - 1)
                        else:
                            pe.wait_ge(s_sel, 1)
                            slot_tokens(1).then_inc(s_idx_mm, 1)
                if next_rows:
                    pe.wait_ge(s_xg[1 - par], 16 * ST * (i + 1))
                    rows_transposed(1 - par).then_inc(s_xT_mm, 1)
                    if gather_next:
                        pe.wait_ge(s_sel, e + 2)
                        slot_tokens(par).then_inc(s_idx_mm, 1)
                else:
                    for t in range(ST):
                        for g in range(NG):
                            n = GROUP[g]
                            last = pe.transpose(bank[0:SLOT_T, (5, 7)[t], :].bitcast(BF16)[:, g * 128:g * 128 + n],
                                                sel[0:n, par, g, t * SLOT_T:(t + 1) * SLOT_T], ident_b[0:n, 0:n])
                    last.then_inc(s_selT_mm, 1)
                pe.wait_ge(s_w2[par], 16 * (i + 1))
                for m in range(DT):
                    for t in range(MT):
                        if m == 0:
                            pe.wait_ge(s_hid, MT * e + t + 1)
                        out_bank, c0 = (4, m * SLOTS) if next_rows else (LAST_Y_BANK[m], 0)
                        last = pe.matmul(bank[:, out_bank, c0:c0 + width], w2_sb[:, par, t, m * 128:(m + 1) * 128],
                                         hid[:, t, 0:width], start=(t == 0), stop=(t == MT - 1))
                    if m == DT - 1 or not next_rows:
                        last.then_inc(s_y_mm, 1)

            def narrowest(tokens, widths, work):
                if len(widths) == 1:
                    work(widths[0])
                else:
                    with pe.If(tokens > widths[0]):
                        narrowest(tokens, widths[1:], work)
                    with pe.Else():
                        work(widths[0])

            def expert(i, par, gather_next, next_rows, prev):
                e = 2 * i + par
                tokens = pe.value_load(count[0:1, bass.ds(e, 1)], min_val=0, max_val=TOK)
                narrowest(tokens, WIDTHS, lambda width: products(i, par, gather_next, next_rows, prev, width))

            expert(0, 0, True, True, False)
            expert(0, 1, True, True, True)
            with pe.Fori(1, LAST_PAIR) as i:
                for par in range(2):
                    expert(i, par, True, True, True)
            expert(LAST_PAIR, 0, False, True, True)
            expert(LAST_PAIR, 1, False, False, True)
            pe.wait_ge(s_selT, 1)
            pe.wait_ge(s_yr, E - 1)
            for m in range(DT):
                pe.wait_ge(s_y, E + m)
                for t in range(ST):
                    last = pe.transpose(bank[0:SLOT_T, LAST_ROW_BANK[t], m * 128:(m + 1) * 128],
                                        yT[:, m, t * SLOT_T:(t + 1) * SLOT_T], ident)
                    if m == DT - 1:
                        last.then_inc(s_yT_mm, 1)

            with further_passes(pe):
                with pe.Fori(0, E * MORE) as n:
                    pe.wait_ge(o_sel, n + 1)
                    slot_tokens(0).then_inc(o_idx_mm, 1)
                    pe.wait_ge(o_xg, 16 * ST * (n + 1))
                    rows_transposed(0).then_inc(o_xT_mm, 1)
                    pe.wait_ge(o_x, n + 1)
                    pe.wait_ge(o_w, 48 * (n + 1))
                    for m in range(MT):
                        if m >= 4:
                            pe.wait_ge(o_hid, MT * n + m - 3)
                        gate_up(0, m, xT[:, 0], SLOTS).then_inc(o_gu_mm, 1)
                    pe.wait_ge(o_hid, MT * n + MT)
                    for m in range(DT):
                        for t in range(MT):
                            last = pe.matmul(bank[:, 4, m * SLOTS:(m + 1) * SLOTS], w2_sb[:, 0, t, m * 128:(m + 1) * 128],
                                             hid[:, t, :], start=(t == 0), stop=(t == MT - 1))
                    last.then_inc(o_y_mm, 1)
                    pe.wait_ge(o_y, n + 1)
                    y_rows().then_inc(o_yT_mm, 1)
                    pe.wait_ge(o_yr, n + 1)

            for g in range(NG):
                n = GROUP[g]
                if g >= 4:
                    pe.wait_ge(s_mix2, g - 3)
                for t in range(ST):
                    if g == 0:
                        pe.wait_ge(s_yr, E + t)
                    last = pe.matmul(bank[0:n, g % 4, 0:D], selT[:, t, g, 0:n], y_sb[:, 1, t, :], start=(t == 0), stop=(t == ST - 1))
                last.then_inc(s_last_mm, 1)

        @block.scalar
        def _(act):
            def load_table(func, use):
                act.activation(unread[0:1, use:use + 1], eps_col[0:1, :], func)

            def values_in(j):
                act.wait_ge(s_v_mm, j + 1)
                for g in (2 * j, 2 * j + 1):
                    n = GROUP[g]
                    last = act.activation(v_sb[0:n, g, :], bank[0:n, VALUE_BANK[j], (g % 2) * D:(g % 2 + 1) * D], ACT.Copy)
                last.then_inc(s_v, 1)

            def probs(g):
                n = GROUP[g]
                act.wait_ge(s_neg_top, g + 1)
                act.activation(prob[0:n, g, 0:n], score[0:n, g, 0:n], ACT.Exp, bias=neg_top[0:n, g:g + 1],
                               accum_out=prob_sum[0:n, g:g + 1]).then_inc(s_prob, 1)

            def probT_in(g):
                n = GROUP[g]
                act.wait_ge(s_probT_mm, g + 1)
                if g >= 2:
                    act.wait_ge(s_attn_mm, g - 1)
                act.activation(probT[0:n, g % 2, 0:n], bank[0:n, PROB_BANK[g % 2], 0:n], ACT.Copy).then_inc(s_probT, 1)

            def root(g, mv_ready, done):
                n = GROUP[g]
                act.wait_ge(mv_ready, g + 1)
                act.activation(std[0:n, g:g + 1], mv[0:n, g, 1:2], ACT.Sqrt, bias=eps_col[0:n, :]).then_inc(done, 1)

            def normalise(g, source, target, ready, done):
                n = GROUP[g]
                act.wait_ge(ready, g + 1)
                act.activation(target[0:n, g, :], source[0:n, g, :], ACT.Identity, scale=rstd[0:n, g:g + 1],
                               bias=shift[0:n, g:g + 1]).then_inc(done, 1)

            def h1T_in(g):
                n = GROUP[g]
                act.wait_ge(s_h1T_mm, g + 1)
                act.activation(h1T[:, g, :, 0:n], bank[:, H1T_BANK[g % 2], 0:DT * 128].rearrange("p (m t) -> p m t", m=DT)[:, :, 0:n],
                               ACT.Copy).then_inc(s_h1T, 1)

            act.wait_ge(s_const, 1)
            load_table(ACT.Exp, 0)
            act.wait_ge(s_vf_w_mm, 1)
            act.activation(vf_w[:].rearrange("p m d -> p (m d)"), bank[:, 4, :], ACT.Copy).then_inc(s_vf_w, 1)
            probs(0)
            probs(1)
            values_in(0)
            probs(2)
            probs(3)
            probT_in(0)
            probs(4)
            probs(5)
            probT_in(1)
            load_table(ACT.Sqrt, 1)
            values_in(1)
            for g in range(NG + 3):
                if g + 2 < NG:
                    probT_in(g + 2)
                if 1 <= g <= NG:
                    root(g - 1, s_mv, s_std)
                if g == 2:
                    values_in(2)
                if 2 <= g < NG + 2 and g - 2 not in BY_VECTOR:
                    normalise(g - 2, pre, h1, s_shift, s_h1)
                if 3 <= g:
                    h1T_in(g - 3)
            act.wait_ge(s_std, NG)
            load_table(ACT.Silu, 2)
            act.wait_ge(s_x0_mm, 1)
            act.activation(xT[:, 0, 1, :], bank[:, 6, 0:SLOTS], ACT.Copy).then_inc(s_x0, 1)

            def y_in(e):
                act.wait_ge(s_y_mm, e + 1)
                act.activation(yT[:].rearrange("p m t -> p (m t)"), bank[:, 4, 0:DT * SLOTS], ACT.Copy).then_inc(s_y, 1)

            def rows_in(e, par, stored):
                act.wait_ge(s_yT_mm, e + 1)
                if stored is not None:
                    act.wait_ge(s_y_dram[par], 16 * stored)
                act.activation(y_sb[:, par].rearrange("p t d -> p (t d)"), bank[0:SLOT_T, 6, :], ACT.Copy).then_inc(s_yr, 1)

            def expert(i, par, prev, stored):
                e = 2 * i + par
                for m in range(MT):
                    act.wait_ge(s_gu_mm, MT * e + m + 1)
                    if prev or m >= 2:
                        act.wait_ge(s_hid, MT * e + m - 1)
                    act.activation(gated[:, m % 2, :], bank[:, m % 4, 0:SLOTS], ACT.Silu).then_inc(s_silu, 1)
                    if m == 1 and prev:
                        rows_in(e - 1, 1 - par, stored)

            expert(0, 0, False, None)
            act.wait_ge(s_setup, 4)
            y_in(0)
            expert(0, 1, True, None)
            y_in(1)
            with act.Fori(1, LAST_PAIR) as i:
                expert(i, 0, True, i - 1)
                y_in(2 * i)
                expert(i, 1, True, i)
                y_in(2 * i + 1)
            expert(LAST_PAIR, 0, True, LAST_PAIR - 1)
            y_in(E - 2)
            act.wait_ge(s_gap, 1)
            act.activation(tanh_gap[:], gap[:], ACT.Tanh, scale=0.5).then_inc(s_tanh, 1)
            expert(LAST_PAIR, 1, True, LAST_PAIR)
            act.wait_ge(s_selT_mm, 1)
            for t in range(ST):
                for g0, g1, n in ((0, NG - 1, GT), (NG - 1, NG, GROUP[NG - 1])):
                    last = act.activation(selT[:, t, g0:g1, 0:n],
                                          bank[0:SLOT_T, (5, 7)[t], :].bitcast(BF16)[:, g0 * 128:g1 * 128].rearrange("p (g c) -> p g c", c=128)[:, :, 0:n],
                                          ACT.Copy)
            last.then_inc(s_selT, 1)
            for m in range(DT):
                act.wait_ge(s_y_mm, E + m)
                act.activation(yT[:, m, :], bank[:, LAST_Y_BANK[m], 0:SLOTS], ACT.Copy).then_inc(s_y, 1)
            act.wait_ge(s_y_dram[1], 16 * LAST_PAIR)
            for t in range(ST):
                act.wait_ge(s_yT_mm, E + t)
                act.activation(y_sb[:, 1, t, :], bank[0:SLOT_T, LAST_ROW_BANK[t], 0:D], ACT.Copy).then_inc(s_yr, 1)

            with further_passes(act):
                all_stored(act)
                with act.Fori(0, E * MORE) as n:
                    for m in range(MT):
                        act.wait_ge(o_gu_mm, MT * n + m + 1)
                        if m >= 2:
                            act.wait_ge(o_hid, MT * n + m - 1)
                        act.activation(gated[:, m % 2, :], bank[:, m % 4, 0:SLOTS], ACT.Silu).then_inc(o_silu, 1)
                    act.wait_ge(o_y_mm, n + 1)
                    act.activation(yT[:].rearrange("p m t -> p (m t)"), bank[:, 4, 0:DT * SLOTS], ACT.Copy).then_inc(o_y, 1)
                    act.wait_ge(o_yT_mm, n + 1)
                    act.activation(y_sb[:, 0].rearrange("p t d -> p (t d)"), bank[0:SLOT_T, 6, :], ACT.Copy).then_inc(o_yr, 1)
                    act.wait_ge(o_y_dram, 16 * (n + 1))

            for g in range(NG + 1):
                if g < NG:
                    root(g, s_mv2, s_std2)
                if g >= 1 and g - 1 not in BY_VECTOR:
                    normalise(g - 1, mix2, out_sb, s_shift2, s_out)

        @block.vector
        def _(dve):
            linked = [0]

            def link(ins):
                linked[0] += 1
                ins.then_inc(s_link, 1)
                dve.wait_ge(s_link, linked[0])

            dve.memset(warm_b[:], 0.0).then_inc(s_warm, 1)
            dve.memset(eps_col[:], EPS).then_inc(s_const, 1)
            dve.wait_ge(s_small, 32)
            pos_v = vec[:, V_POS:V_POS + DT * T].rearrange("p (m j) -> p m j", m=DT)
            dve.tensor_tensor(posb[:, :, 1:T], pos_v[:, :, 1:T],
                              vec[:, V_BT:V_BT + DT].unsqueeze(2).broadcast_to([128, DT, NP]), ALU.add)
            link(dve.tensor_tensor(posb[:, :, 0:1], pos_v[:, :, 0:1], vec[:, V_CLS:V_CLS + DT].unsqueeze(2), ALU.add))
            dve.tensor_copy(tri_b[:], cst[0:GT, C_TRI:C_TRI + GT]).then_inc(s_const, 1)
            dve.tensor_copy(lower[:].rearrange("p e f -> p (e f)"), cst[0:GT, C_LT:C_LT + E * E])
            dve.tensor_copy(ident_b[:], cst[0:GT, C_ID:C_ID + GT]).then_inc(s_const, 1)
            dve.tensor_copy(tid_b[:].rearrange("p g c -> p (g c)"), cst[0:GT, C_TID:C_TID + 2 * NG])
            dve.tensor_copy(bv_b[:], vec[:, V_BV:V_BV + DT].unsqueeze(2).broadcast_to([128, DT, GT])).then_inc(s_const, 1)
            dve.tensor_copy(hT[:].rearrange("p m (b j) -> p m b j", j=T)[:, :, :, 0],
                            posb[:, :, 0:1].broadcast_to([128, DT, B])).then_inc(s_hT, 1)
            for half in range(2):
                dve.wait_ge(s_patch_mm, half + 1)
                for m in range(DT):
                    dve.tensor_tensor(per_image(hT[:, m, half * HALF_T:(half + 1) * HALF_T], T)[:, :, 1:T],
                                      per_image(bank[:, 2 * half + m, 0:HALF_P], NP),
                                      posb[:, m, 1:T].unsqueeze(1).broadcast_to([128, HALF_B, NP]), ALU.add).then_inc(s_hT, 1)

            def rope(half, w):
                n = 2 * half + w
                dve.wait_ge(s_qk_mm, n + 1)
                if n >= 2:
                    dve.wait_ge(s_rope, n - 1)
                b0 = 4 * (1 - half) + 2 * w
                for j, (eo, table) in enumerate(((0, cos8), (1, sin8), (1, cos8), (0, sin8))):
                    last = dve.scalar_tensor_tensor(out=per_image(rope_t[:, n % 2, j, :], T), in0=per_image(bank[:, b0 + eo, 0:HALF_T], T),
                                                    scalar=vec[:, (V_BQ, V_BK)[w] + eo:(V_BQ, V_BK)[w] + eo + 1],
                                                    in1=table, op0=ALU.add, op1=ALU.mult)
                last.then_inc(s_rope_mul, 1)

            def masked(g):
                n = GROUP[g]
                dve.wait_ge(s_score_mm, g // 2 + 1)
                dve.tensor_tensor_reduce(out=score[0:n, g, 0:n], in0=bank[0:n, SCORE_BANK[g // 2], (g % 2) * 128:(g % 2) * 128 + n],
                                         in1=mask[0:n, 0:n], scale=1.0 / np.sqrt(D), scalar=-3e38, op0=ALU.add, op1=ALU.max,
                                         accum_out=top[0:n, g:g + 1]).then_inc(s_score, 1)

            def negated(g):
                n = GROUP[g]
                dve.wait_ge(s_score, g + 1)
                dve.tensor_scalar(neg_top[0:n, g:g + 1], top[0:n, g:g + 1], -1.0, None, ALU.mult).then_inc(s_neg_top, 1)

            def rows_in(g):
                n = GROUP[g]
                dve.wait_ge(s_row_mm, g // 2 + 1)
                dve.tensor_tensor(resid[0:n, g, :], bank[0:n, ROW_BANK[g // 2], (g % 2) * D:(g % 2 + 1) * D], bias_rows[0:n, :],
                                  ALU.add).then_inc(s_resid, 1)

            for w in range(2):
                rope(0, w)
            for w in range(2):
                rope(1, w)
            def one_over_sum(g):
                n = GROUP[g]
                dve.wait_ge(s_prob, g + 1)
                dve.reciprocal(prob_inv[0:n, g:g + 1], prob_sum[0:n, g:g + 1]).then_inc(s_prob_inv, 1)

            dve.wait_ge(s_cb_mm, 1)
            dve.wait_ge(s_bias, 32)
            dve.tensor_tensor(bias_rows[:], bank[0:GT, 6, 0:D], bf_rows[:], ALU.add).then_inc(s_cb, 1)
            for j in range(NG // 2):
                for g in (2 * j, 2 * j + 1):
                    masked(g)
                for g in (2 * j, 2 * j + 1):
                    negated(g)
                if j == 0:
                    dve.wait_ge(s_cb, 1)
                    for g in range(2):
                        rows_in(g)
            one_over_sum(0)
            one_over_sum(1)

            def residual(g, total, summed):
                n = GROUP[g]
                dve.wait_ge(summed, g + 1)
                dve.bn_stats(stats[0:n, g, :], total[0:n, g, :]).then_inc(s_link, 1)
                linked[0] += 1

            def aggregate(g, done):
                dve.wait_ge(s_link, linked[0])
                dve.bn_aggr(mv[0:GROUP[g], g, :], stats[0:GROUP[g], g, :]).then_inc(done, 1)

            def one_over_std(g, std_ready, inverted):
                n = GROUP[g]
                dve.wait_ge(std_ready, g + 1)
                dve.reciprocal(rstd[0:n, g:g + 1], std[0:n, g:g + 1]).then_inc(inverted, 1)

            def attention_in(g):
                n = GROUP[g]
                dve.wait_ge(s_attn_mm, g + 1)
                dve.wait_ge(s_prob_inv, g + 1)
                dve.wait_ge(s_resid, g + 1)
                dve.scalar_tensor_tensor(out=pre[0:n, g, :], in0=bank[0:n, ATTN_BANK[g % 2], 0:D], scalar=prob_inv[0:n, g:g + 1],
                                         in1=resid[0:n, g, :], op0=ALU.mult, op1=ALU.add).then_inc(s_pre, 1)

            for g in range(NG):
                attention_in(g)
                if g >= 1:
                    aggregate(g - 1, s_mv)
                residual(g, pre, s_pre)
                if g in (0, 1):
                    for late in (2 * g + 2, 2 * g + 3):
                        rows_in(late)
                        one_over_sum(late)
                if g >= 1:
                    one_over_std(g - 1, s_std, s_rstd)
            aggregate(NG - 1, s_mv)

            def normalise(g, source, target, ready, done):
                n = GROUP[g]
                dve.wait_ge(ready, g + 1)
                dve.tensor_scalar(target[0:n, g, :], source[0:n, g, :], mv[0:n, g, 0:1], rstd[0:n, g:g + 1],
                                  ALU.subtract, ALU.mult).then_inc(done, 1)

            normalise(BY_VECTOR[0], pre, h1, s_rstd, s_h1_late)
            one_over_std(NG - 1, s_std, s_rstd)
            normalise(BY_VECTOR[1], pre, h1, s_rstd, s_h1_late)

            def route(b):
                g0, g1 = BATCHES[b]
                dve.wait_ge(s_logit_mm, b + 1)
                whole = g1 - 1 if g1 == NG else g1
                last = dve.tensor_copy(logit[:, g0:whole, :], bank[0:GT, LOGIT_BANK[b], 0:(whole - g0) * E].rearrange("p (g e) -> p g e", e=E))
                if g1 == NG:
                    n = GROUP[whole]
                    last = dve.tensor_copy(logit[0:n, whole, :], bank[0:n, LOGIT_BANK[b], (whole - g0) * E:(g1 - g0) * E])
                link(last)
                shape = [GT, g1 - g0, E, E]
                other, own = logit[:, g0:g1, :].unsqueeze(2).broadcast_to(shape), logit[:, g0:g1, :].unsqueeze(3).broadcast_to(shape)
                dve.tensor_tensor(above[:, g0:g1], other, own, ALU.is_gt)
                link(dve.tensor_tensor(equal[:, g0:g1], other, own, ALU.is_equal))
                link(dve.tensor_tensor(equal[:, g0:g1], equal[:, g0:g1], lower[:].unsqueeze(1).broadcast_to(shape), ALU.mult))
                link(dve.tensor_tensor(above[:, g0:g1], above[:, g0:g1], equal[:, g0:g1], ALU.add))
                link(dve.tensor_reduce(rank[:, g0:g1, :], above[:, g0:g1], AX_X, ALU.add))
                dve.tensor_scalar(picked_b[:, g0:g1, :], rank[:, g0:g1, :], 1.5, None, ALU.is_lt).then_inc(s_picked, 1)

            def places(b):
                g0, g1 = BATCHES[b]
                dve.wait_ge(s_pos_mm, b + 1)
                dve.scalar_tensor_tensor(out=place[:, g0:g1, :], in0=bank[0:GT, AHEAD_BANK[b], 0:(g1 - g0) * E].rearrange("p (g e) -> p g e", e=E),
                                         scalar=1.0, in1=picked_b[:, g0:g1, :], op0=ALU.add, op1=ALU.mult).then_inc(s_place, 1)

            dve.wait_ge(s_setup, 4)
            route(0)
            places(0)

            def select_first(b):
                for g in range(*BATCHES[b]):
                    dve.tensor_scalar(sel0[:, g, :], iota, place[:, g, 0:1], None, ALU.is_equal).then_inc(s_sel0, 1)

            def select(e, par, groups):
                for g in groups:
                    last = dve.tensor_scalar(sel[:, par, g, :], iota, place[:, g, bass.ds(e, 1)], None, ALU.is_equal)
                return last

            def slot_index(par, done):
                numbers = bank[0:SLOT_T, 7, 0:2 * ST].rearrange("p (t c) -> p t c", c=2)
                with whole_numbers():
                    return dve.tensor_reduce(tok_idx[:, par, :, 0], numbers, AX_X, ALU.add).then_inc(done, 1)

            def rows_to_sbuf(e, par):
                dve.wait_ge(s_xT_mm, e)
                dve.tensor_copy(xT[:, par].rearrange("p k t -> p (k t)"), bank[:, 5, 0:DT * SLOTS]).then_inc(s_x, 1)

            dve.wait_ge(s_rope, 4)
            dve.wait_ge(s_place, 1)
            select_first(0)
            route(1)
            places(1)
            dve.wait_ge(s_place, 2)
            select_first(1)
            link(dve.tensor_copy(count_f[:], bank[0:1, AHEAD_BANK[1], (REST - 1) * E:REST * E]))
            dve.tensor_copy(count[:], count_f[:])
            with whole_numbers():
                dve.reduce_max(most[0:1, 0:1], count_f[:], AX_X).then_inc(s_count, 1)
            dve.wait_ge(s_x0_mm, 1)
            dve.tensor_copy(xT[:, 0, 0, :], bank[:, 5, 0:SLOTS]).then_inc(s_x0, 1)
            select(1, 1, range(NG)).then_inc(s_sel, 1)
            dve.wait_ge(s_idx_mm, 1)
            slot_index(1, s_idx)

            def expert(i, par, gather_next, next_rows):
                e = 2 * i + par
                for m in range(MT):
                    dve.wait_ge(s_silu, MT * e + m + 1)
                    dve.tensor_tensor(hid[:, m, :], gated[:, m % 2, :], bank[:, m % 4, SLOTS:2 * SLOTS], ALU.mult).then_inc(s_hid, 1)
                    if gather_next and m == 3:
                        select(e + 2, par, range(NG)).then_inc(s_sel, 1)
                if next_rows:
                    rows_to_sbuf(e + 1, 1 - par)
                if gather_next:
                    dve.wait_ge(s_idx_mm, e + 2)
                    slot_index(par, s_idx)

            with dve.Fori(0, LAST_PAIR) as i:
                for par in range(2):
                    expert(i, par, True, True)

            dve.tensor_scalar(first[:], rank[:], 0.5, None, ALU.is_lt)
            link(dve.tensor_scalar(picked[:], rank[:], 1.5, None, ALU.is_lt))
            link(dve.tensor_tensor(second[:], picked[:], first[:], ALU.subtract))
            dve.tensor_tensor(pick_t[:, 4], logit[:], first[:], ALU.mult)
            link(dve.tensor_tensor(pick_t[:, 5], logit[:], second[:], ALU.mult))
            dve.tensor_reduce(l1[:], pick_t[:, 4], AX_X, ALU.add)
            link(dve.tensor_reduce(l2[:], pick_t[:, 5], AX_X, ALU.add))
            dve.tensor_tensor(gap[:], l1[:], l2[:], ALU.subtract).then_inc(s_gap, 1)
            shape = [GT, NG, E, E]
            link(dve.tensor_tensor(equal[:], picked[:].unsqueeze(2).broadcast_to(shape), lower[:].unsqueeze(1).broadcast_to(shape), ALU.mult))
            link(dve.tensor_reduce(high[:], equal[:], AX_X, ALU.add))
            link(dve.tensor_tensor(high[:], high[:], picked[:], ALU.mult))
            link(dve.tensor_tensor(low[:], picked[:], high[:], ALU.subtract))
            dve.memset(early[:], 0.0)
            dve.tensor_tensor(row_of[:], place[:], row0.unsqueeze(1).broadcast_to([GT, NG, E]), ALU.add)
            link(dve.tensor_scalar(row_early[:], place[:], float(SLOTS), None, ALU.is_le))
            link(dve.tensor_tensor(row_early[:], row_early[:], row_of[:], ALU.mult))
            dve.tensor_copy(early[:, 0, :, 0:E - 2], low[:, :, 0:E - 2])
            dve.tensor_copy(early[:, 1, :, 0:E - 2], high[:, :, 0:E - 2])
            link(dve.tensor_copy(early[:, 1, :, E - 2:E - 1], picked[:, :, E - 2:E - 1]))
            for c in range(1, PASSES):
                link(dve.tensor_scalar(pos1[:], place[:], float(c * SLOTS), float(PASS_ROWS - SLOTS), ALU.is_gt, ALU.mult))
                link(dve.tensor_tensor(row_of[:], row_of[:], pos1[:], ALU.add))
            for k, which in enumerate((low, high)):
                dve.tensor_tensor(pick_t[:, k], row_of[:], which[:], ALU.mult)
                last = dve.tensor_tensor(pick_t[:, 2 + k], row_early[:], early[:, k], ALU.mult)
            link(last)
            with whole_numbers():
                dve.tensor_reduce(row_idx[:], pick_t[:, 0:2], AX_X, ALU.add)
                dve.tensor_reduce(early_idx[:], pick_t[:, 2:4], AX_X, ALU.add).then_inc(s_rows, 1)

            expert(LAST_PAIR, 0, False, True)

            dve.wait_ge(s_tanh, 1)
            dve.wait_ge(s_rows, 1)
            shape = [GT, NG, E]
            dve.tensor_scalar(choice_w[:, 0, :], tanh_gap[:], 0.5, 0.5, ALU.mult, ALU.add)
            link(dve.tensor_scalar(choice_w[:, 1, :], tanh_gap[:], -0.5, 0.5, ALU.mult, ALU.add))
            dve.tensor_tensor(weight_t[:, 0], first[:], choice_w[:, 0, :].unsqueeze(2).broadcast_to(shape), ALU.mult)
            link(dve.tensor_tensor(weight_t[:, 1], second[:], choice_w[:, 1, :].unsqueeze(2).broadcast_to(shape), ALU.mult))
            link(dve.tensor_tensor(expert_w[:], weight_t[:, 0], weight_t[:, 1], ALU.add))
            for k, which in enumerate((early[:, 0], early[:, 1], low[:], high[:])):
                last = dve.tensor_tensor(weighted_t[:, k], expert_w[:], which, ALU.mult)
            link(last)
            dve.tensor_copy(last_w[:], expert_w[:, :, E - 1])
            link(dve.tensor_reduce(pair_w[:], weighted_t[:], AX_X, ALU.add))

            expert(LAST_PAIR, 1, False, False)

            def sum_early(arrived0, arrived, partly, done):
                for g in range(NG):
                    n = GROUP[g]
                    dve.wait_ge(arrived0[g], 16)
                    dve.scalar_tensor_tensor(out=mix2[0:n, g, :], in0=y_tok[0:n, 0, g, :], scalar=pair_w[0:n, 0, g:g + 1],
                                             in1=h1[0:n, g, :], op0=ALU.mult, op1=ALU.add).then_inc(partly, 1)
                for g in range(NG):
                    n = GROUP[g]
                    dve.wait_ge(partly, g + 1)
                    dve.wait_ge(arrived[g], 16)
                    dve.scalar_tensor_tensor(out=mix[0:n, g, :], in0=y_tok[0:n, 1, g, :], scalar=pair_w[0:n, 1, g:g + 1],
                                             in1=mix2[0:n, g, :], op0=ALU.mult, op1=ALU.add).then_inc(done, 1)

            sum_early(s_y_tok0, s_y_tok, s_partly, s_mix)

            with further_passes(dve):
                all_stored(dve)
                with dve.Fori(0, E) as e:
                    for c in range(MORE):
                        n = e * MORE + c
                        dve.tensor_scalar(pos1[:, :, 0], place[:, :, bass.ds(e, 1)].rearrange("p g o -> p (g o)"),
                                          -float(SLOTS * (c + 1)), None, ALU.add).then_inc(o_slot, 1)
                        dve.wait_ge(o_slot, n + 1)
                        dve.tensor_tensor(sel[:, 0], iota.unsqueeze(1).broadcast_to([GT, NG, SLOTS]),
                                          pos1[:, :, 0:1].broadcast_to([GT, NG, SLOTS]), ALU.is_equal).then_inc(o_sel, 1)
                        dve.wait_ge(o_idx_mm, n + 1)
                        slot_index(0, o_idx)
                        dve.wait_ge(o_xT_mm, n + 1)
                        dve.tensor_copy(xT[:, 0].rearrange("p k t -> p (k t)"), bank[:, 5, 0:DT * SLOTS]).then_inc(o_x, 1)
                        for m in range(MT):
                            dve.wait_ge(o_silu, MT * n + m + 1)
                            dve.tensor_tensor(hid[:, m, :], gated[:, m % 2, :], bank[:, m % 4, SLOTS:2 * SLOTS],
                                              ALU.mult).then_inc(o_hid, 1)
                        dve.wait_ge(o_yr, n + 1)
                dve.wait_ge(o_y_tok, 32 * NG)
                dve.tensor_copy(pair_w[:, 0:2, :], pair_w[:, 2:4, :]).then_inc(o_slot, 1)
                dve.memset(last_w[:], 0.0).then_inc(o_slot, 1)
                dve.wait_ge(o_slot, E * MORE + 2)
                dve.wait_ge(s_mix, NG)
                sum_early((o_y_tok,) * NG, (o_y_tok,) * NG, o_partly, o_mix)
                dve.wait_ge(o_mix, NG)

            for g in range(NG):
                n = GROUP[g]
                dve.wait_ge(s_last_mm, g + 1)
                dve.wait_ge(s_mix, g + 1)
                dve.scalar_tensor_tensor(out=mix2[0:n, g, :], in0=bank[0:n, g % 4, 0:D], scalar=last_w[0:n, g:g + 1],
                                         in1=mix[0:n, g, :], op0=ALU.mult, op1=ALU.add).then_inc(s_mix2, 1)
                if g >= 1:
                    aggregate(g - 1, s_mv2)
                if g >= 2:
                    one_over_std(g - 2, s_std2, s_rstd2)
                residual(g, mix2, s_mix2)
            one_over_std(NG - 2, s_std2, s_rstd2)
            aggregate(NG - 1, s_mv2)
            normalise(BY_VECTOR[0], mix2, out_sb, s_rstd2, s_out_late)
            one_over_std(NG - 1, s_std2, s_rstd2)
            normalise(BY_VECTOR[1], mix2, out_sb, s_rstd2, s_out_late)


def kernel(x, L0_tok_W, L0_tok_b, L0_tok_class_token, L0_tok_pos_embedding, L0_attn_Wq, L0_attn_bq, L0_attn_Wk,
           L0_attn_bk, L0_attn_Wv, L0_attn_bv, L0_attn_Wf, L0_attn_bf, L0_ffn_gate, L0_ffn_experts_w1,
           L0_ffn_experts_w2, L0_ffn_experts_w3):
    import concourse.bacc as bacc
    from concourse.bass_utils import run_bass_kernel_spmd

    def tiles(a):
        return a.reshape(-1, 128, a.shape[-1]).transpose(1, 0, 2)

    def columns(a):
        return np.asarray(a).reshape(DT, 128).T

    x = np.asarray(x)
    pt = x.reshape(B, CH, GRID, PATCH, GRID, PATCH).transpose(1, 3, 5, 0, 2, 4).reshape(KP // 2, 2, 128, 2, HALF_P)
    pt = pt.transpose(3, 0, 2, 1, 4)
    tw = np.asarray(L0_tok_W).T.reshape(KP // 2, 2, 128, D).transpose(0, 2, 1, 3)
    order = np.concatenate([np.arange(0, D, 2), np.arange(1, D, 2)])
    aw = np.stack([tiles(np.asarray(L0_attn_Wq)[order].T), tiles(np.asarray(L0_attn_Wk)[order].T),
                   tiles(np.asarray(L0_attn_Wv)), tiles(np.asarray(L0_attn_Wf).T)], axis=1)
    pos = np.asarray(L0_tok_pos_embedding).reshape(T, DT, 128).transpose(2, 1, 0).reshape(128, DT * T)
    vecs = np.concatenate([columns(np.asarray(L0_attn_bq)[order]), columns(np.asarray(L0_attn_bk)[order]),
                           columns(L0_tok_b), columns(np.asarray(L0_tok_class_token).reshape(D)), columns(L0_attn_bv), pos], axis=1)

    def up(w):
        return np.asarray(w).reshape(E, DT, 128, INNER).transpose(0, 2, 1, 3).reshape(E, 128, DT * INNER)

    arrays = {
        "patches": pt, "tok_w": tw, "vecs": vecs, "attn_w": aw, "bf": np.asarray(L0_attn_bf),
        "gate": tiles(np.asarray(L0_ffn_gate)), "w1": up(L0_ffn_experts_w1), "w3": up(L0_ffn_experts_w3),
        "w2": np.asarray(L0_ffn_experts_w2).reshape(E, MT, 128, D).transpose(0, 2, 1, 3), "consts": shape_constants(),
    }
    arrays = {k: np.ascontiguousarray(v) for k, v in arrays.items()}
    nc = bacc.Bacc("TRN2", target_bir_lowering=False, num_devices=1)
    args = [nc.dram_tensor(k, v.shape, mybir.dt.from_np(v.dtype), kind="ExternalInput").ap() for k, v in arrays.items()]
    out = nc.dram_tensor("out", (B, T, D), F32, kind="ExternalOutput").ap()
    vit_layer(nc, *args, out)
    r = run_bass_kernel_spmd(nc, [arrays], core_ids=[0])
    return r.results[0]["out"]
```
